# Optimizing a Trainium2 kernel written in Bass

```python
import numpy as np
import jax
import jax.numpy as jnp

def _softmax(x, axis=-1):
    return jax.nn.softmax(x, axis=axis)

def _gelu(x):
    return jax.nn.gelu(x, approximate=True)

def _silu(x):
    return jax.nn.silu(x)

def _sigmoid(x):
    return jax.nn.sigmoid(x)

def _layernorm(x, axis=-1, eps=1e-05):
    m = jnp.mean(x, axis=axis, keepdims=True)
    v = jnp.var(x, axis=axis, keepdims=True)
    return (x - m) / jnp.sqrt(v + eps)

def _scatter_add(tgt, idx, src, axis=0):
    return tgt.at[idx].add(src)

def _segment_sum(src, seg, n):
    return jax.ops.segment_sum(src, seg, n)
kernel_name = 'mk_seq_postln_d4_jaxref_r8_19e0b3'

def setup_inputs(seed: int=0):
    np.random.seed(seed)
    _w = jnp.asarray

    def _L0_attn_setup():
        import jax, jax.numpy as jnp
        import numpy as np
        L, B, S, D, H, HID = (6, 4, 128, 128, 16, 512)
        HD = D // H

        def _pos_encoding(S, D):
            pos = np.arange(S)
            level = np.frexp((pos + 1).astype(np.float64))[1] - 1
            coord = (pos >> level) / 2.0 ** level
            div = np.exp(np.arange(0, D, 2, dtype=np.float64) * -(np.log(10000.0) / D))
            ang = pos[:, None].astype(np.float64) * div[None, :]
            pe = np.zeros((S, D), np.float32)
            pe[:, 0::2] = (np.sin(ang) * coord[:, None]).astype(np.float32)
            pe[:, 1::2] = (np.cos(ang) * coord[:, None]).astype(np.float32)
            return jnp.asarray(pe)

        def _sierpinski_mask(S):
            i = np.arange(S)
            return jnp.asarray((np.bitwise_and(i[:, None], i[None, :]) == 0).astype(np.float32))

        def _ln(h, g, b, eps=1e-05):
            m = h.mean(-1, keepdims=True)
            v = h.var(-1, keepdims=True)
            return (h - m) * jax.lax.rsqrt(v + eps) * g + b
        key = jax.random.key(seed)
        ks = iter(jax.random.split(key, 16))
        w = lambda k, shape: 0.02 * jax.random.normal(k, shape, jnp.float32)
        return {'x': jax.random.normal(next(ks), (B, S, D), jnp.float32), 'Wq': w(next(ks), (L, D, D)), 'bq': jnp.zeros((L, D), jnp.float32), 'Wk': w(next(ks), (L, D, D)), 'bk': jnp.zeros((L, D), jnp.float32), 'Wv': w(next(ks), (L, D, D)), 'bv': jnp.zeros((L, D), jnp.float32), 'Wo': w(next(ks), (L, D, D)), 'bo': jnp.zeros((L, D), jnp.float32), 'W1': w(next(ks), (L, D, HID)), 'b1': jnp.zeros((L, HID), jnp.float32), 'W2': w(next(ks), (L, HID, D)), 'b2': jnp.zeros((L, D), jnp.float32), 'ln1_g': jnp.ones((L, D), jnp.float32), 'ln1_b': jnp.zeros((L, D), jnp.float32), 'ln2_g': jnp.ones((L, D), jnp.float32), 'ln2_b': jnp.zeros((L, D), jnp.float32), 'lnf_g': jnp.ones((D,), jnp.float32), 'lnf_b': jnp.zeros((D,), jnp.float32)}
    _L0_attn_in = _L0_attn_setup()

    def _L0_ffn_setup():
        import jax, jax.numpy as jnp
        import numpy as np
        D_MODEL = 128
        N_EXPERTS = 8
        TOP_K = 2
        HIDDEN = 4 * D_MODEL
        key = jax.random.key(seed)
        ks = jax.random.split(key, 6)
        B, S = (2, 256)
        x = jax.random.normal(ks[0], (B, S, D_MODEL), dtype=jnp.float32)
        shared_w1 = jax.random.normal(ks[1], (HIDDEN, D_MODEL), dtype=jnp.float32) * 0.02
        shared_w2 = jax.random.normal(ks[2], (D_MODEL, HIDDEN), dtype=jnp.float32) * 0.02
        experts_w1 = jax.random.normal(ks[3], (N_EXPERTS, HIDDEN, D_MODEL), dtype=jnp.float32) * 0.02
        experts_w2 = jax.random.normal(ks[4], (N_EXPERTS, D_MODEL, HIDDEN), dtype=jnp.float32) * 0.02
        gate_w = jax.random.normal(ks[5], (N_EXPERTS, D_MODEL), dtype=jnp.float32) * 0.02
        return {'x': x, 'shared_w1': shared_w1, 'shared_w2': shared_w2, 'experts_w1': experts_w1, 'experts_w2': experts_w2, 'gate_w': gate_w}
    _L0_ffn_in = _L0_ffn_setup()

    def _L1_attn_setup():
        import jax, jax.numpy as jnp
        import numpy as np
        B, S, D, H = (2, 512, 128, 16)
        HD = D // H
        KCONV = 4

        def _rmsnorm(x, scale, eps=1e-06):
            return x * jax.lax.rsqrt(jnp.mean(x * x, axis=-1, keepdims=True) + eps) * scale

        def _l2norm(x, eps=1e-06):
            return x * jax.lax.rsqrt(jnp.sum(x * x, axis=-1, keepdims=True) + eps)

        def _causal_dwconv_silu(x, w):
            k = w.shape[1]
            s = x.shape[1]
            xp = jnp.pad(x, ((0, 0), (k - 1, 0), (0, 0)))
            out = sum((xp[:, i:i + s, :] * w[:, i] for i in range(k)))
            return jax.nn.silu(out)

        def _p20_scan(x, decay_log, theta):
            b, s, d = x.shape
            xc = x.reshape(b, s, d // 2, 2)
            u = jax.lax.complex(xc[..., 0], xc[..., 1])
            a = jnp.exp(-jnp.exp(decay_log)) * jnp.exp(1j * theta)

            def step(carry, u_t):
                st = carry * a + u_t
                return (st, st)
            _, ys = jax.lax.scan(step, jnp.zeros((b, d // 2), u.dtype), jnp.swapaxes(u, 0, 1))
            ys = jnp.swapaxes(ys, 0, 1)
            return jnp.stack([ys.real, ys.imag], axis=-1).reshape(b, s, d)

        def _gated_delta_rule(q, k, v, g, beta):
            scale = q.shape[-1] ** (-0.5)
            q = _l2norm(q)
            k = _l2norm(k)
            qt, kt, vt = (jnp.moveaxis(t, 1, 0) for t in (q, k, v))
            gt, bt = (jnp.moveaxis(t, 1, 0) for t in (g, beta))
            s0 = jnp.zeros((q.shape[0], q.shape[2], q.shape[3], v.shape[3]), v.dtype)

            def step(state, inp):
                q_t, k_t, v_t, g_t, b_t = inp
                state = state * jnp.exp(g_t)[..., None, None]
                v_err = (v_t - jnp.einsum('bhkv,bhk->bhv', state, k_t)) * b_t[..., None]
                state = state + jnp.einsum('bhk,bhv->bhkv', k_t, v_err)
                o_t = jnp.einsum('bhkv,bhk->bhv', state, q_t) * scale
                return (state, o_t)
            _, o = jax.lax.scan(step, s0, (qt, kt, vt, gt, bt))
            return jnp.moveaxis(o, 0, 1)
        key = jax.random.key(seed)
        ks = jax.random.split(key, 16)
        w = lambda k, shp, s=0.02: jax.random.normal(k, shp, jnp.float32) * s
        ctrl_out = 3 * D + 2 * H + D
        ctrl_b = jnp.concatenate([jnp.zeros((3 * D,), jnp.float32), jnp.full((H,), 1.5, jnp.float32), jnp.full((H,), -2.0, jnp.float32), jnp.full((D,), -1.5, jnp.float32)])

        def conv_w(k):
            base = jnp.zeros((D, KCONV), jnp.float32).at[:, -1].set(1.0)
            return base + w(k, (D, KCONV), 0.02)
        return {'hidden': jax.random.normal(ks[0], (B, S, D), jnp.float32), 'p20_decay_log': w(ks[1], (D // 2,), 1.0), 'p20_theta': jax.random.uniform(ks[2], (D // 2,), jnp.float32, 0.0, 2.0 * np.pi), 'ctrl_W': w(ks[3], (D, ctrl_out)), 'ctrl_b': ctrl_b, 'p20c_W': w(ks[4], (D, 3 * D), 0.001), 'qconv_w': conv_w(ks[5]), 'kconv_w': conv_w(ks[6]), 'vconv_w': conv_w(ks[7]), 'mnorm_scale': jnp.ones((HD,), jnp.float32), 'vnorm_scale': jnp.ones((D,), jnp.float32), 'ramp_logit': jnp.full((D,), -4.595, jnp.float32), 'out_W': w(ks[8], (2 * D, D), 0.02), 'out_b': jnp.zeros((D,), jnp.float32)}
    _L1_attn_in = _L1_attn_setup()

    def _L1_ffn_setup():
        import jax, jax.numpy as jnp
        import numpy as np
        BLOCK = 16
        _GRID = jnp.array([0.0, 0.5, 1.0, 1.5, 2.0, 3.0, 4.0, 6.0], dtype=jnp.float32)
        _MID = jnp.array([0.25, 0.75, 1.25, 1.75, 2.5, 3.5, 5.0], dtype=jnp.float32)

        def fp4_quant_dequant(x):
            shape = x.shape
            xb = x.reshape(shape[:-1] + (shape[-1] // BLOCK, BLOCK))
            scale = jnp.max(jnp.abs(xb), axis=-1, keepdims=True) / 6.0
            scale = jnp.maximum(scale, jnp.float32(1e-12))
            xn = xb / scale
            idx = jnp.searchsorted(_MID, jnp.abs(xn))
            q = _GRID[idx] * jnp.sign(xn) * scale
            return q.reshape(shape)

        def fp4_linear(x, w):
            xq = fp4_quant_dequant(x)
            wq = fp4_quant_dequant(w)
            return jnp.einsum('bsk,nk->bsn', xq, wq)
        key = jax.random.key(seed)
        k1, k2, k3, k4 = jax.random.split(key, 4)
        H, I = (128, 352)
        x = jax.random.normal(k1, (4, 512, H), dtype=jnp.float32)
        w_gate = jax.random.normal(k2, (I, H), dtype=jnp.float32) * 0.02
        w_up = jax.random.normal(k3, (I, H), dtype=jnp.float32) * 0.02
        w_down = jax.random.normal(k4, (H, I), dtype=jnp.float32) * 0.02
        return {'x': x, 'w_gate': w_gate, 'w_up': w_up, 'w_down': w_down}
    _L1_ffn_in = _L1_ffn_setup()

    def _L2_attn_setup():
        import jax, jax.numpy as jnp
        import numpy as np
        D = 128
        H = 16
        HKV = 4
        HD = D // H
        L = 64
        EPS = 1e-06
        LN_EPS = 1e-05
        B, S = (2, 128)

        def _feat(x):
            return jax.nn.elu(x) + 1.0
        key = jax.random.key(seed)
        ks = jax.random.split(key, 8)
        w = lambda k, shape: jax.random.normal(k, shape, jnp.float32) * 0.02
        return {'x': jax.random.normal(ks[0], (B, S, D), jnp.float32), 'Wq': w(ks[1], (D, D)), 'bq': jnp.zeros((D,), jnp.float32), 'Wk': w(ks[2], (D, HKV * HD)), 'bk': jnp.zeros((HKV * HD,), jnp.float32), 'Wv': w(ks[3], (D, HKV * HD)), 'bv': jnp.zeros((HKV * HD,), jnp.float32), 'Wc': w(ks[4], (HKV * HD, L)), 'We': w(ks[5], (L, HKV * HD)), 'Wo': w(ks[6], (D, D)), 'bo': jnp.zeros((D,), jnp.float32), 'gamma': jnp.ones((D,), jnp.float32), 'beta': jnp.zeros((D,), jnp.float32)}
    _L2_attn_in = _L2_attn_setup()

    def _L2_ffn_setup():
        import jax, jax.numpy as jnp
        import numpy as np
        D_IN, D_HID = (128, 512)

        def _ternary(key, shape):
            return jax.random.randint(key, shape, -1, 2).astype(jnp.float32)

        def _tlin(x, w, s):
            return jnp.einsum('bsi,oi->bso', x, w) * s
        key = jax.random.key(seed)
        ks = jax.random.split(key, 12)
        inv = lambda fan: 1.0 / np.sqrt(fan).astype(np.float32)
        return {'x': jax.random.normal(ks[0], (4, 256, D_IN), dtype=jnp.float32), 'w1_w': _ternary(ks[1], (D_HID, D_IN)), 'w1_s': jax.random.uniform(ks[2], (D_HID,), dtype=jnp.float32) * inv(D_IN), 'w2_w': _ternary(ks[3], (D_HID, D_IN)), 'w2_s': jax.random.uniform(ks[4], (D_HID,), dtype=jnp.float32) * inv(D_IN), 'h1_w': _ternary(ks[5], (D_HID, D_HID)), 'h1_s': jax.random.uniform(ks[6], (D_HID,), dtype=jnp.float32) * inv(D_HID), 'h2_w': _ternary(ks[7], (D_HID, D_HID)), 'h2_s': jax.random.uniform(ks[8], (D_HID,), dtype=jnp.float32) * inv(D_HID), 'w3_w': _ternary(ks[9], (D_IN, D_HID)), 'w3_s': jax.random.uniform(ks[10], (D_IN,), dtype=jnp.float32) * inv(D_HID)}
    _L2_ffn_in = _L2_ffn_setup()

    def _L3_attn_setup():
        import jax, jax.numpy as jnp
        import numpy as np
        D_MODEL = 128
        NUM_HEADS = 16
        D_K = D_MODEL // NUM_HEADS
        THETA = 10000.0

        def apply_rope(x, positions):
            half = D_K // 2
            inv_freq = THETA ** (-jnp.arange(half, dtype=jnp.float32) * 2.0 / D_K)
            angles = positions[:, None, :, None].astype(jnp.float32) * inv_freq
            cos, sin = (jnp.cos(angles), jnp.sin(angles))
            x1 = x[..., 0::2]
            x2 = x[..., 1::2]
            out_even = x1 * cos - x2 * sin
            out_odd = x1 * sin + x2 * cos
            out = jnp.stack([out_even, out_odd], axis=-1)
            return out.reshape(x.shape)
        key = jax.random.key(seed)
        ks = jax.random.split(key, 5)
        b, s = (2, 256)
        scale = 0.02
        return {'x': jax.random.normal(ks[0], (b, s, D_MODEL), dtype=jnp.float32), 'Wq': jax.random.normal(ks[1], (D_MODEL, D_MODEL), dtype=jnp.float32) * scale, 'Wk': jax.random.normal(ks[2], (D_MODEL, D_MODEL), dtype=jnp.float32) * scale, 'Wv': jax.random.normal(ks[3], (D_MODEL, D_MODEL), dtype=jnp.float32) * scale, 'Wo': jax.random.normal(ks[4], (D_MODEL, D_MODEL), dtype=jnp.float32) * scale}
    _L3_attn_in = _L3_attn_setup()

    def _L3_ffn_setup():
        import jax, jax.numpy as jnp
        import numpy as np
        B, N, D = (4, 256, 128)
        SPARSITY = 0.01
        key = jax.random.key(seed)
        k1, k2, k3 = jax.random.split(key, 3)
        x = jax.random.normal(k1, (B, N, D), dtype=jnp.float32)
        spatial = jax.random.normal(k2, (D, D), dtype=jnp.float32) * 0.02
        freq = jnp.fft.fft(spatial, axis=-1)
        k = int(D * SPARSITY)
        mag = jnp.abs(freq)
        kth = jax.lax.top_k(mag, k)[0][:, -1:]
        w_sparse = jnp.where(mag >= kth, freq, 0.0 + 0j)
        bias = jax.random.normal(k3, (D,), dtype=jnp.float32) * 0.01
        return {'x': x, 'w_freq_real': jnp.real(w_sparse).astype(jnp.float32), 'w_freq_imag': jnp.imag(w_sparse).astype(jnp.float32), 'bias': bias}
    _L3_ffn_in = _L3_ffn_setup()
    _d = {'L0_attn_x': _L0_attn_in['x'], 'L0_attn_Wq': _L0_attn_in['Wq'], 'L0_attn_bq': _L0_attn_in['bq'], 'L0_attn_Wk': _L0_attn_in['Wk'], 'L0_attn_bk': _L0_attn_in['bk'], 'L0_attn_Wv': _L0_attn_in['Wv'], 'L0_attn_bv': _L0_attn_in['bv'], 'L0_attn_Wo': _L0_attn_in['Wo'], 'L0_attn_bo': _L0_attn_in['bo'], 'L0_attn_W1': _L0_attn_in['W1'], 'L0_attn_b1': _L0_attn_in['b1'], 'L0_attn_W2': _L0_attn_in['W2'], 'L0_attn_b2': _L0_attn_in['b2'], 'L0_attn_ln1_g': _L0_attn_in['ln1_g'], 'L0_attn_ln1_b': _L0_attn_in['ln1_b'], 'L0_attn_ln2_g': _L0_attn_in['ln2_g'], 'L0_attn_ln2_b': _L0_attn_in['ln2_b'], 'L0_attn_lnf_g': _L0_attn_in['lnf_g'], 'L0_attn_lnf_b': _L0_attn_in['lnf_b'], 'L0_ffn_shared_w1': _L0_ffn_in['shared_w1'], 'L0_ffn_shared_w2': _L0_ffn_in['shared_w2'], 'L0_ffn_experts_w1': _L0_ffn_in['experts_w1'], 'L0_ffn_experts_w2': _L0_ffn_in['experts_w2'], 'L0_ffn_gate_w': _L0_ffn_in['gate_w'], 'L1_attn_p20_decay_log': _L1_attn_in['p20_decay_log'], 'L1_attn_p20_theta': _L1_attn_in['p20_theta'], 'L1_attn_ctrl_W': _L1_attn_in['ctrl_W'], 'L1_attn_ctrl_b': _L1_attn_in['ctrl_b'], 'L1_attn_p20c_W': _L1_attn_in['p20c_W'], 'L1_attn_qconv_w': _L1_attn_in['qconv_w'], 'L1_attn_kconv_w': _L1_attn_in['kconv_w'], 'L1_attn_vconv_w': _L1_attn_in['vconv_w'], 'L1_attn_mnorm_scale': _L1_attn_in['mnorm_scale'], 'L1_attn_vnorm_scale': _L1_attn_in['vnorm_scale'], 'L1_attn_ramp_logit': _L1_attn_in['ramp_logit'], 'L1_attn_out_W': _L1_attn_in['out_W'], 'L1_attn_out_b': _L1_attn_in['out_b'], 'L1_ffn_w_gate': _L1_ffn_in['w_gate'], 'L1_ffn_w_up': _L1_ffn_in['w_up'], 'L1_ffn_w_down': _L1_ffn_in['w_down'], 'L2_attn_Wq': _L2_attn_in['Wq'], 'L2_attn_bq': _L2_attn_in['bq'], 'L2_attn_Wk': _L2_attn_in['Wk'], 'L2_attn_bk': _L2_attn_in['bk'], 'L2_attn_Wv': _L2_attn_in['Wv'], 'L2_attn_bv': _L2_attn_in['bv'], 'L2_attn_Wc': _L2_attn_in['Wc'], 'L2_attn_We': _L2_attn_in['We'], 'L2_attn_Wo': _L2_attn_in['Wo'], 'L2_attn_bo': _L2_attn_in['bo'], 'L2_attn_gamma': _L2_attn_in['gamma'], 'L2_attn_beta': _L2_attn_in['beta'], 'L2_ffn_w1_w': _L2_ffn_in['w1_w'], 'L2_ffn_w1_s': _L2_ffn_in['w1_s'], 'L2_ffn_w2_w': _L2_ffn_in['w2_w'], 'L2_ffn_w2_s': _L2_ffn_in['w2_s'], 'L2_ffn_h1_w': _L2_ffn_in['h1_w'], 'L2_ffn_h1_s': _L2_ffn_in['h1_s'], 'L2_ffn_h2_w': _L2_ffn_in['h2_w'], 'L2_ffn_h2_s': _L2_ffn_in['h2_s'], 'L2_ffn_w3_w': _L2_ffn_in['w3_w'], 'L2_ffn_w3_s': _L2_ffn_in['w3_s'], 'L3_attn_Wq': _L3_attn_in['Wq'], 'L3_attn_Wk': _L3_attn_in['Wk'], 'L3_attn_Wv': _L3_attn_in['Wv'], 'L3_attn_Wo': _L3_attn_in['Wo'], 'L3_ffn_w_freq_real': _L3_ffn_in['w_freq_real'], 'L3_ffn_w_freq_imag': _L3_ffn_in['w_freq_imag'], 'L3_ffn_bias': _L3_ffn_in['bias']}
    _x0 = _d['L0_attn_x']
    _d['L0_attn_x'] = jax.random.normal(jax.random.fold_in(jax.random.key(seed), 1), (16, 256, 128), dtype=_x0.dtype)
    del _x0
    return _d

def reference(L0_attn_x, L0_attn_Wq, L0_attn_bq, L0_attn_Wk, L0_attn_bk, L0_attn_Wv, L0_attn_bv, L0_attn_Wo, L0_attn_bo, L0_attn_W1, L0_attn_b1, L0_attn_W2, L0_attn_b2, L0_attn_ln1_g, L0_attn_ln1_b, L0_attn_ln2_g, L0_attn_ln2_b, L0_attn_lnf_g, L0_attn_lnf_b, L0_ffn_shared_w1, L0_ffn_shared_w2, L0_ffn_experts_w1, L0_ffn_experts_w2, L0_ffn_gate_w, L1_attn_p20_decay_log, L1_attn_p20_theta, L1_attn_ctrl_W, L1_attn_ctrl_b, L1_attn_p20c_W, L1_attn_qconv_w, L1_attn_kconv_w, L1_attn_vconv_w, L1_attn_mnorm_scale, L1_attn_vnorm_scale, L1_attn_ramp_logit, L1_attn_out_W, L1_attn_out_b, L1_ffn_w_gate, L1_ffn_w_up, L1_ffn_w_down, L2_attn_Wq, L2_attn_bq, L2_attn_Wk, L2_attn_bk, L2_attn_Wv, L2_attn_bv, L2_attn_Wc, L2_attn_We, L2_attn_Wo, L2_attn_bo, L2_attn_gamma, L2_attn_beta, L2_ffn_w1_w, L2_ffn_w1_s, L2_ffn_w2_w, L2_ffn_w2_s, L2_ffn_h1_w, L2_ffn_h1_s, L2_ffn_h2_w, L2_ffn_h2_s, L2_ffn_w3_w, L2_ffn_w3_s, L3_attn_Wq, L3_attn_Wk, L3_attn_Wv, L3_attn_Wo, L3_ffn_w_freq_real, L3_ffn_w_freq_imag, L3_ffn_bias):

    def _L0_attn_ref(x, Wq, bq, Wk, bk, Wv, bv, Wo, bo, W1, b1, W2, b2, ln1_g, ln1_b, ln2_g, ln2_b, lnf_g, lnf_b):
        import jax, jax.numpy as jnp
        import numpy as np
        L, B, S, D, H, HID = (6, 4, 128, 128, 16, 512)
        HD = D // H

        def _pos_encoding(S, D):
            pos = np.arange(S)
            level = np.frexp((pos + 1).astype(np.float64))[1] - 1
            coord = (pos >> level) / 2.0 ** level
            div = np.exp(np.arange(0, D, 2, dtype=np.float64) * -(np.log(10000.0) / D))
            ang = pos[:, None].astype(np.float64) * div[None, :]
            pe = np.zeros((S, D), np.float32)
            pe[:, 0::2] = (np.sin(ang) * coord[:, None]).astype(np.float32)
            pe[:, 1::2] = (np.cos(ang) * coord[:, None]).astype(np.float32)
            return jnp.asarray(pe)

        def _sierpinski_mask(S):
            i = np.arange(S)
            return jnp.asarray((np.bitwise_and(i[:, None], i[None, :]) == 0).astype(np.float32))

        def _ln(h, g, b, eps=1e-05):
            m = h.mean(-1, keepdims=True)
            v = h.var(-1, keepdims=True)
            return (h - m) * jax.lax.rsqrt(v + eps) * g + b
        Bx, Sx, Dx = x.shape
        smask = _sierpinski_mask(Sx)
        h = x + _pos_encoding(Sx, Dx)
        scale = 1.0 / jnp.sqrt(jnp.float32(HD))

        def layer(h, p):
            wq, bq_, wk, bk_, wv, bv_, wo, bo_, w1, b1_, w2, b2_, g1, be1, g2, be2 = p
            q = (h @ wq + bq_).reshape(Bx, Sx, H, HD).transpose(0, 2, 1, 3)
            k = (h @ wk + bk_).reshape(Bx, Sx, H, HD).transpose(0, 2, 1, 3)
            v = (h @ wv + bv_).reshape(Bx, Sx, H, HD).transpose(0, 2, 1, 3)
            scores = jnp.einsum('bhqd,bhkd->bhqk', q, k) * scale
            scores = scores * smask
            a = jax.nn.softmax(scores, axis=-1)
            att = jnp.einsum('bhqk,bhkd->bhqd', a, v)
            att = att.transpose(0, 2, 1, 3).reshape(Bx, Sx, Dx) @ wo + bo_
            h = _ln(h + att, g1, be1)
            ff = jax.nn.gelu(h @ w1 + b1_, approximate=False) @ w2 + b2_
            h = _ln(h + ff, g2, be2)
            return (h, None)
        params = (Wq, bq, Wk, bk, Wv, bv, Wo, bo, W1, b1, W2, b2, ln1_g, ln1_b, ln2_g, ln2_b)
        h, _ = jax.lax.scan(layer, h, params)
        return _ln(h, lnf_g, lnf_b)

    def _L0_ffn_ref(x, shared_w1, shared_w2, experts_w1, experts_w2, gate_w):
        import jax, jax.numpy as jnp
        import numpy as np
        D_MODEL = 128
        N_EXPERTS = 8
        TOP_K = 2
        HIDDEN = 4 * D_MODEL
        B, S, D = x.shape
        T = B * S
        x_flat = x.reshape(T, D)
        shared = jnp.einsum('td,dh->th', x_flat, shared_w1.T)
        shared = jnp.einsum('th,hd->td', jax.nn.silu(shared), shared_w2.T)
        gate_logits = x_flat @ gate_w.T
        top_k_gates, top_k_idx = jax.lax.top_k(gate_logits, TOP_K)
        top_k_gates = jax.nn.softmax(top_k_gates, axis=1)
        gates = jnp.zeros((T, N_EXPERTS), dtype=x.dtype)
        gates = gates.at[jnp.arange(T)[:, None], top_k_idx].set(top_k_gates)
        h = jnp.einsum('td,ehd->teh', x_flat, experts_w1)
        expert_out = jnp.einsum('teh,edh->ted', jax.nn.silu(h), experts_w2)
        selected = jnp.einsum('ted,te->td', expert_out, gates)
        return (shared + selected).reshape(B, S, D)

    def _L1_attn_ref(hidden, p20_decay_log, p20_theta, ctrl_W, ctrl_b, p20c_W, qconv_w, kconv_w, vconv_w, mnorm_scale, vnorm_scale, ramp_logit, out_W, out_b):
        import jax, jax.numpy as jnp
        import numpy as np
        B, S, D, H = (2, 512, 128, 16)
        HD = D // H
        KCONV = 4

        def _rmsnorm(x, scale, eps=1e-06):
            return x * jax.lax.rsqrt(jnp.mean(x * x, axis=-1, keepdims=True) + eps) * scale

        def _l2norm(x, eps=1e-06):
            return x * jax.lax.rsqrt(jnp.sum(x * x, axis=-1, keepdims=True) + eps)

        def _causal_dwconv_silu(x, w):
            k = w.shape[1]
            s = x.shape[1]
            xp = jnp.pad(x, ((0, 0), (k - 1, 0), (0, 0)))
            out = sum((xp[:, i:i + s, :] * w[:, i] for i in range(k)))
            return jax.nn.silu(out)

        def _p20_scan(x, decay_log, theta):
            b, s, d = x.shape
            xc = x.reshape(b, s, d // 2, 2)
            u = jax.lax.complex(xc[..., 0], xc[..., 1])
            a = jnp.exp(-jnp.exp(decay_log)) * jnp.exp(1j * theta)

            def step(carry, u_t):
                st = carry * a + u_t
                return (st, st)
            _, ys = jax.lax.scan(step, jnp.zeros((b, d // 2), u.dtype), jnp.swapaxes(u, 0, 1))
            ys = jnp.swapaxes(ys, 0, 1)
            return jnp.stack([ys.real, ys.imag], axis=-1).reshape(b, s, d)

        def _gated_delta_rule(q, k, v, g, beta):
            scale = q.shape[-1] ** (-0.5)
            q = _l2norm(q)
            k = _l2norm(k)
            qt, kt, vt = (jnp.moveaxis(t, 1, 0) for t in (q, k, v))
            gt, bt = (jnp.moveaxis(t, 1, 0) for t in (g, beta))
            s0 = jnp.zeros((q.shape[0], q.shape[2], q.shape[3], v.shape[3]), v.dtype)

            def step(state, inp):
                q_t, k_t, v_t, g_t, b_t = inp
                state = state * jnp.exp(g_t)[..., None, None]
                v_err = (v_t - jnp.einsum('bhkv,bhk->bhv', state, k_t)) * b_t[..., None]
                state = state + jnp.einsum('bhk,bhv->bhkv', k_t, v_err)
                o_t = jnp.einsum('bhkv,bhk->bhv', state, q_t) * scale
                return (state, o_t)
            _, o = jax.lax.scan(step, s0, (qt, kt, vt, gt, bt))
            return jnp.moveaxis(o, 0, 1)
        b, s, d = hidden.shape
        p20_read = _p20_scan(hidden, p20_decay_log, p20_theta)
        normed_p20 = _rmsnorm(p20_read, vnorm_scale)
        p20_q, p20_k, p20_v = jnp.split(normed_p20 @ p20c_W, 3, axis=-1)
        ramp = jax.nn.sigmoid(ramp_logit)
        ctrl = hidden @ ctrl_W + ctrl_b
        q_in, k_in, v_in, dec_in, beta_in, gate_in = jnp.split(ctrl, np.cumsum([d, d, d, H, H]).tolist(), axis=-1)
        q_in = _causal_dwconv_silu(q_in, qconv_w)
        k_in = _causal_dwconv_silu(k_in, kconv_w)
        v_in = _causal_dwconv_silu(v_in, vconv_w)
        queries = (q_in + ramp * p20_q).reshape(b, s, H, HD)
        keys = (k_in + ramp * p20_k).reshape(b, s, H, HD)
        values = (v_in + ramp * p20_v).reshape(b, s, H, HD)
        g = jax.nn.log_sigmoid(dec_in.astype(jnp.float32)).astype(hidden.dtype)
        beta = jax.nn.sigmoid(beta_in)
        reads = _gated_delta_rule(queries, keys, values, g, beta)
        normed_reads = _rmsnorm(reads, mnorm_scale).reshape(b, s, d)
        fused = jnp.concatenate([normed_reads, normed_p20], axis=-1)
        projected = fused @ out_W + out_b
        return jax.nn.sigmoid(gate_in) * projected

    def _L1_ffn_ref(x, w_gate, w_up, w_down):
        import jax, jax.numpy as jnp
        import numpy as np
        BLOCK = 16
        _GRID = jnp.array([0.0, 0.5, 1.0, 1.5, 2.0, 3.0, 4.0, 6.0], dtype=jnp.float32)
        _MID = jnp.array([0.25, 0.75, 1.25, 1.75, 2.5, 3.5, 5.0], dtype=jnp.float32)

        def fp4_quant_dequant(x):
            shape = x.shape
            xb = x.reshape(shape[:-1] + (shape[-1] // BLOCK, BLOCK))
            scale = jnp.max(jnp.abs(xb), axis=-1, keepdims=True) / 6.0
            scale = jnp.maximum(scale, jnp.float32(1e-12))
            xn = xb / scale
            idx = jnp.searchsorted(_MID, jnp.abs(xn))
            q = _GRID[idx] * jnp.sign(xn) * scale
            return q.reshape(shape)

        def fp4_linear(x, w):
            xq = fp4_quant_dequant(x)
            wq = fp4_quant_dequant(w)
            return jnp.einsum('bsk,nk->bsn', xq, wq)
        gate = fp4_linear(x, w_gate)
        y = fp4_linear(x, w_up)
        h = jax.nn.silu(gate) * y
        return fp4_linear(h, w_down)

    def _L2_attn_ref(x, Wq, bq, Wk, bk, Wv, bv, Wc, We, Wo, bo, gamma, beta):
        import jax, jax.numpy as jnp
        import numpy as np
        D = 128
        H = 16
        HKV = 4
        HD = D // H
        L = 64
        EPS = 1e-06
        LN_EPS = 1e-05
        B, S = (2, 128)

        def _feat(x):
            return jax.nn.elu(x) + 1.0
        b, s, _ = x.shape
        residual = x
        q = x @ Wq + bq
        k = x @ Wk + bk
        v = x @ Wv + bv
        k = k @ Wc @ We
        v = v @ Wc @ We
        q = q.reshape(b, s, H, HD).transpose(0, 2, 1, 3)
        k = k.reshape(b, s, HKV, HD).transpose(0, 2, 1, 3)
        v = v.reshape(b, s, HKV, HD).transpose(0, 2, 1, 3)
        rep = H // HKV
        k = jnp.repeat(k, rep, axis=1)
        v = jnp.repeat(v, rep, axis=1)
        qf = _feat(q)
        kf = _feat(k)
        kv = jnp.einsum('bhsf,bhsd->bhsfd', kf, v)
        kv_cum = jnp.cumsum(kv, axis=2)
        num = jnp.einsum('bhsf,bhsfd->bhsd', qf, kv_cum)
        den = jnp.einsum('bhsf,bhsf->bhs', qf, jnp.cumsum(kf, axis=2))[..., None] + EPS
        o = num / den
        o = o.transpose(0, 2, 1, 3).reshape(b, s, D)
        o = o @ Wo + bo
        y = residual + o
        mu = jnp.mean(y, axis=-1, keepdims=True)
        var = jnp.var(y, axis=-1, keepdims=True)
        return (y - mu) / jnp.sqrt(var + LN_EPS) * gamma + beta

    def _L2_ffn_ref(x, w1_w, w1_s, w2_w, w2_s, h1_w, h1_s, h2_w, h2_s, w3_w, w3_s):
        import jax, jax.numpy as jnp
        import numpy as np
        D_IN, D_HID = (128, 512)

        def _ternary(key, shape):
            return jax.random.randint(key, shape, -1, 2).astype(jnp.float32)

        def _tlin(x, w, s):
            return jnp.einsum('bsi,oi->bso', x, w) * s
        h = jax.nn.silu(_tlin(x, w1_w, w1_s)) * _tlin(x, w2_w, w2_s)
        h = jax.nn.gelu(_tlin(h, h1_w, h1_s), approximate=False)
        h = jax.nn.gelu(_tlin(h, h2_w, h2_s), approximate=False)
        return _tlin(h, w3_w, w3_s)

    def _L3_attn_ref(x, Wq, Wk, Wv, Wo):
        import jax, jax.numpy as jnp
        import numpy as np
        D_MODEL = 128
        NUM_HEADS = 16
        D_K = D_MODEL // NUM_HEADS
        THETA = 10000.0

        def apply_rope(x, positions):
            half = D_K // 2
            inv_freq = THETA ** (-jnp.arange(half, dtype=jnp.float32) * 2.0 / D_K)
            angles = positions[:, None, :, None].astype(jnp.float32) * inv_freq
            cos, sin = (jnp.cos(angles), jnp.sin(angles))
            x1 = x[..., 0::2]
            x2 = x[..., 1::2]
            out_even = x1 * cos - x2 * sin
            out_odd = x1 * sin + x2 * cos
            out = jnp.stack([out_even, out_odd], axis=-1)
            return out.reshape(x.shape)
        b, s, _ = x.shape
        Q = x @ Wq.T
        K = x @ Wk.T
        V = x @ Wv.T
        split = lambda t: t.reshape(b, s, NUM_HEADS, D_K).transpose(0, 2, 1, 3)
        Q, K, V = (split(Q), split(K), split(V))
        positions = jnp.broadcast_to(jnp.arange(s, dtype=jnp.int32), (b, s))
        Q = apply_rope(Q, positions)
        K = apply_rope(K, positions)
        scores = jnp.einsum('bhqd,bhkd->bhqk', Q, K) / jnp.sqrt(jnp.float32(D_K))
        causal = jnp.tril(jnp.ones((s, s), dtype=bool))
        scores = jnp.where(causal[None, None], scores, -jnp.inf)
        attn = jax.nn.softmax(scores, axis=-1)
        out = jnp.einsum('bhqk,bhkd->bhqd', attn, V)
        out = out.transpose(0, 2, 1, 3).reshape(b, s, D_MODEL)
        return out @ Wo.T

    def _L3_ffn_ref(x, w_freq_real, w_freq_imag, bias):
        import jax, jax.numpy as jnp
        import numpy as np
        B, N, D = (4, 256, 128)
        SPARSITY = 0.01
        w = jax.lax.complex(w_freq_real, w_freq_imag)
        x_freq = jnp.fft.fft(x, axis=-1)
        y_freq = jnp.einsum('bnd,do->bno', x_freq, w)
        y = jnp.real(jnp.fft.ifft(y_freq, axis=-1))
        return y + bias
    x = L0_attn_x
    x = _layernorm(x + _L0_attn_ref(x, L0_attn_Wq, L0_attn_bq, L0_attn_Wk, L0_attn_bk, L0_attn_Wv, L0_attn_bv, L0_attn_Wo, L0_attn_bo, L0_attn_W1, L0_attn_b1, L0_attn_W2, L0_attn_b2, L0_attn_ln1_g, L0_attn_ln1_b, L0_attn_ln2_g, L0_attn_ln2_b, L0_attn_lnf_g, L0_attn_lnf_b), axis=-1)
    x = _layernorm(x + _L0_ffn_ref(x, L0_ffn_shared_w1, L0_ffn_shared_w2, L0_ffn_experts_w1, L0_ffn_experts_w2, L0_ffn_gate_w), axis=-1)
    x = _layernorm(x + _L1_attn_ref(x, L1_attn_p20_decay_log, L1_attn_p20_theta, L1_attn_ctrl_W, L1_attn_ctrl_b, L1_attn_p20c_W, L1_attn_qconv_w, L1_attn_kconv_w, L1_attn_vconv_w, L1_attn_mnorm_scale, L1_attn_vnorm_scale, L1_attn_ramp_logit, L1_attn_out_W, L1_attn_out_b), axis=-1)
    x = _layernorm(x + _L1_ffn_ref(x, L1_ffn_w_gate, L1_ffn_w_up, L1_ffn_w_down), axis=-1)
    x = _layernorm(x + _L2_attn_ref(x, L2_attn_Wq, L2_attn_bq, L2_attn_Wk, L2_attn_bk, L2_attn_Wv, L2_attn_bv, L2_attn_Wc, L2_attn_We, L2_attn_Wo, L2_attn_bo, L2_attn_gamma, L2_attn_beta), axis=-1)
    x = _layernorm(x + _L2_ffn_ref(x, L2_ffn_w1_w, L2_ffn_w1_s, L2_ffn_w2_w, L2_ffn_w2_s, L2_ffn_h1_w, L2_ffn_h1_s, L2_ffn_h2_w, L2_ffn_h2_s, L2_ffn_w3_w, L2_ffn_w3_s), axis=-1)
    x = _layernorm(x + _L3_attn_ref(x, L3_attn_Wq, L3_attn_Wk, L3_attn_Wv, L3_attn_Wo), axis=-1)
    x = _layernorm(x + _L3_ffn_ref(x, L3_ffn_w_freq_real, L3_ffn_w_freq_imag, L3_ffn_bias), axis=-1)
    return x

_drawn_inputs = setup_inputs


def setup_inputs(seed=0):
    import zlib

    import numpy as np

    out = dict(_drawn_inputs(seed))
    spreads = {'L0_attn_bq': (0.0, 0.8),
     'L0_attn_bk': (0.0, 0.8),
     'L0_attn_bv': (0.0, 0.302),
     'L0_attn_bo': (0.0, 0.1),
     'L0_attn_b1': (0.0, 0.1),
     'L0_attn_b2': (0.0, 0.1),
     'L0_attn_ln1_g': (1.0, 0.2),
     'L0_attn_ln1_b': (0.0, 0.1),
     'L0_attn_ln2_g': (1.0, 0.2),
     'L0_attn_ln2_b': (0.0, 0.1),
     'L0_attn_lnf_g': (1.0, 0.2),
     'L0_attn_lnf_b': (0.0, 0.1),
     'L1_attn_mnorm_scale': (1.0, 0.6),
     'L1_attn_vnorm_scale': (1.0, 0.6),
     'L1_attn_ramp_logit': (-4.59499979019165, 0.6),
     'L1_attn_out_b': (0.0, 0.486),
     'L2_attn_bq': (0.0, 0.8),
     'L2_attn_bk': (0.0, 2.0),
     'L2_attn_bv': (0.0, 0.8),
     'L2_attn_bo': (0.0, 0.1),
     'L2_attn_gamma': (1.0, 0.2),
     'L2_attn_beta': (0.0, 0.1)}
    factors = {'L0_attn_Wq': 8.0,
     'L0_attn_Wk': 8.0,
     'L1_attn_p20c_W': 8.0,
     'L1_ffn_w_gate': 5.79,
     'L1_ffn_w_up': 5.655,
     'L1_ffn_w_down': 5.678,
     'L2_attn_Wq': 8.0,
     'L2_attn_Wk': 8.0,
     'L2_attn_Wv': 8.0,
     'L2_attn_Wc': 8.0,
     'L2_attn_We': 8.0,
     'L2_attn_Wo': 8.0,
     'L2_ffn_w1_w': 8.0,
     'L2_ffn_w1_s': 8.0,
     'L2_ffn_w2_w': 8.0,
     'L2_ffn_w2_s': 8.0,
     'L2_ffn_h1_w': 8.0,
     'L2_ffn_h1_s': 8.0,
     'L2_ffn_h2_w': 8.0,
     'L2_ffn_h2_s': 8.0,
     'L2_ffn_w3_w': 8.0,
     'L2_ffn_w3_s': 8.0,
     'L3_attn_Wq': 8.0,
     'L3_attn_Wk': 8.0,
     'L3_attn_Wv': 3.947,
     'L3_attn_Wo': 3.692,
     'L3_ffn_bias': 6.205}
    for name, (base, spread) in spreads.items():
        noise = np.random.default_rng([zlib.crc32(name.encode()), seed]).standard_normal(out[name].shape)
        drawn = base * np.exp(spread * noise) if base else spread * noise
        out[name] = jnp.asarray(drawn.astype(out[name].dtype))
    for name, factor in factors.items():
        out[name] = (out[name] * factor).astype(out[name].dtype)
    return out
```

```python
from contextlib import ExitStack

import numpy as np

import concourse.bass as bass
from concourse import mybir

ALU = mybir.AluOpType
ACT = mybir.ActivationFunctionType
AX_X = mybir.AxisListType.X
F32 = mybir.dt.float32
BF16 = mybir.dt.bfloat16
U32 = mybir.dt.uint32

P = 128
SEQS, S, D = 16, 256, 128
TOKENS = SEQS * S
GROUP = 512
GROUPS = TOKENS // GROUP
TILES = GROUP // P
ds = bass.ds
TWO_PI = (6.28125, float(np.float32(np.float16(2 * np.pi - 6.28125))), float(2 * np.pi - 6.28125 - float(np.float16(2 * np.pi - 6.28125))))


class Ctx:
    pass



def norm_vector(c, dve, nth, rows, rows_ready):
    norm_statistics(c, dve, nth, rows, rows_ready)
    norm_apply(c, dve, nth, rows)


def norm_statistics(c, dve, nth, rows, rows_ready):
    dve.wait_ge(rows_ready[0], rows_ready[1])
    for t in range(TILES):
        last = nc_v(c).bn_stats(c.stats[:, t, :], rows[:, t, :])
    last.then_inc(c.s_stats, 1)
    dve.wait_ge(c.s_stats, nth + 1)
    nc_v(c).memset(c.scratch[:], 0.0)
    for t in range(TILES):
        last = nc_v(c).bn_aggr(c.meanvar[:, t, :], c.stats[:, t, :])
    last.then_inc(c.s_meanvar, 1)
    dve.wait_ge(c.s_meanvar, nth + 1)
    nc_v(c).tensor_scalar(c.vareps[:], c.meanvar[:, :, 1], 1e-5, None, ALU.add).then_inc(c.s_vareps, 1)


def norm_apply(c, dve, nth, rows):
    dve.wait_ge(c.s_rstd, nth + 1)
    for t in range(TILES):
        last = nc_v(c).tensor_scalar(c.normed[:, t, :], rows[:, t, :], c.meanvar[:, t, 0:1], c.rstd[:, t:t + 1],
                                     ALU.subtract, ALU.mult)
    last.then_inc(c.s_normed, 1)


def nc_v(c):
    return c.nc.vector


def norm_pool(c, pool, nth):
    pool.wait_ge(c.s_vareps, nth + 1)
    c.nc.gpsimd.tensor_tensor(c.rstd[:], c.vareps[:], c.minus_half[:], ALU.pow).then_inc(c.s_rstd, 1)


def norm_tensor(c, pe, nth):
    pe.wait_ge(c.s_done, nth + 1)
    pe.wait_ge(c.s_normed, nth + 1)
    for t in range(TILES):
        last = c.nc.tensor.transpose(c.turned[:, t * P:(t + 1) * P], c.normed[:, t, :], c.ident[:])
    last.then_inc(c.s_turned, 1)


def norm_scalar(c, act, nth, at, gain=None, bias=None):
    act.wait_ge(c.s_turned, nth + 1)
    if gain is None:
        c.nc.scalar.activation(c.H[:, at], c.turned[:], ACT.Copy).then_inc(c.s_done, 1)
    else:
        c.nc.scalar.activation(c.H[:, at], c.turned[:], ACT.Identity, bias=bias, scale=gain).then_inc(c.s_done, 1)


def fetch_group(c, pool, nth, i):
    pool.wait_ge(c.s_done, nth + 1)
    c.nc.gpsimd.tensor_copy(c.cur[:], c.H[:, ds(i * GROUP, GROUP)]).then_inc(c.s_cur, 1)


def fetch_ahead(c, dve, i):
    c.nc.vector.tensor_copy(c.cur[:], c.H[:, ds(i * GROUP, GROUP)]).then_inc(c.s_cur, 1)


def over_groups(eng, head, body, tail):
    head(0)
    with eng.Fori(0, GROUPS - 1) as i:
        body(i)
    tail(GROUPS - 1)



def fft_mix(c, base):
    nc = c.nc
    with ExitStack() as ctx:
        def sem(n): return c.sem(n)
        W = load_stage(c, ctx, "s8")
        freq_t = ctx.enter_context(nc.sbuf_tensor("freq_t", [P, 2, P], F32))
        mix = ctx.enter_context(nc.sbuf_tensor("mix", [P, P], F32))
        s_a, s_at, s_m, s_mix, s_rows = sem("fft_a_ready"), sem("fft_at_ready"), sem("fft_m_ready"), sem("fft_mix_ready"), sem("fft_rows_ready")
        bank = c.bank
        block = ctx.enter_context(nc.Block())

        @block.sync
        def _(sp):
            W.start(sp)

        @block.gpsimd
        def _(pool):
            with pool.Fori(0, GROUPS) as i:
                fetch_group(c, pool, i + base, i)
                norm_pool(c, pool, i + base)

        @block.tensor
        def _(pe):
            W.wait(pe)
            nc.tensor.matmul(bank[1][:, 0:P], W["wr"], W["fr"], start=True, stop=False)
            nc.tensor.matmul(bank[1][:, 0:P], W["wi"], W["nfi"], start=False, stop=True)
            nc.tensor.matmul(bank[2][:, 0:P], W["wi"], W["fr"], start=True, stop=False)
            nc.tensor.matmul(bank[2][:, 0:P], W["wr"], W["fi"], start=False, stop=True).then_inc(s_a, 1)
            pe.wait_ge(s_at, 1)
            nc.tensor.matmul(bank[3][:, 0:P], freq_t[:, 0, :], W["gr"], start=True, stop=False)
            nc.tensor.matmul(bank[3][:, 0:P], freq_t[:, 1, :], W["ngi"], start=False, stop=True).then_inc(s_m, 1)
            pe.wait_ge(s_mix, 1)
            with pe.Fori(0, GROUPS) as i:
                pe.wait_ge(c.s_cur, i + (base + 1))
                for t in range(TILES):
                    nc.tensor.matmul(bank[4][:, t * P:(t + 1) * P], c.cur[:, t * P:(t + 1) * P], mix[:], start=True, stop=False)
                    last = nc.tensor.matmul(bank[4][:, t * P:(t + 1) * P], c.ones[0:1, 0:P], W["bias"][0:1], start=False, stop=True)
                last.then_inc(s_rows, 1)
                norm_tensor(c, pe, i + base)

        @block.vector
        def _(dve):
            dve.wait_ge(s_a, 1)
            nc.vector.tensor_copy(freq_t[:, 0, :], bank[1][:, 0:P])
            nc.vector.tensor_copy(freq_t[:, 1, :], bank[2][:, 0:P]).then_inc(s_at, 1)
            dve.wait_ge(s_m, 1)
            nc.vector.tensor_tensor(mix[:], bank[3][:, 0:P], c.ident[:], ALU.add).then_inc(s_mix, 1)
            rows = bank[4][:].rearrange("p (t d) -> p t d", t=TILES)
            with dve.Fori(0, GROUPS) as i:
                norm_vector(c, dve, i + base, rows, (s_rows, i + 1))

        @block.scalar
        def _(act):
            with act.Fori(0, GROUPS) as i:
                norm_scalar(c, act, i + base, ds(i * GROUP, GROUP))
    return base + GROUPS



HEADS, HD, HT = 16, 8, 4
VW = HD + 1
SEQ_G = GROUP // S
JT = S // P
P1 = JT * HT * 2
P2 = HT * 2


class AttentionSems:

    def __init__(self, sem):
        self.s_proj, self.s_qev, self.s_kev = sem("proj_ready"), sem("q_moved"), sem("k_moved")
        self.s_vp, self.s_v = sem("vproj_ready"), sem("v_moved")
        self.s_p1, self.s_mx = sem("scores_ready"), sem("max_taken")
        self.s_negmax, self.s_negpad, self.s_expneg = sem("negmax_ready"), sem("negpad_ready"), sem("expneg_ready")
        self.s_nm, self.s_qaug = sem("negmax_turned"), sem("q_augmented")
        self.s_p2, self.s_e = sem("scores_t_ready"), sem("exp_ready")
        self.s_ot, self.s_o = sem("sums_moved"), sem("sums_turned")
        self.s_pv, self.s_u = sem("pv_ready"), sem("masked_sum_ready")
        self.s_num0, self.s_num, self.s_rec, self.s_att = sem("masked_scaled"), sem("num_ready"), sem("rec_ready"), sem("att_ready")
        self.s_att_t, self.s_att_tm = sem("att_turned"), sem("att_t_moved")
        self.s_rows = sem("rows_ready")


class Attention:
    def __init__(self, c, ctx, tag, causal):
        nc = c.nc
        def sb(n, shape, dt=F32): return ctx.enter_context(nc.sbuf_tensor(tag + n, shape, dt))
        self.c, self.causal = c, causal
        self.q = sb("q", [P, HT, GROUP])
        self.k = sb("k", [P, HT, 4, GROUP])
        self.v = sb("v", [P, TILES, HEADS, 32])
        self.o_t = sb("o_t", [P, HT, S])
        self.mx = sb("mx", [P, JT, HEADS])
        self.negmax = sb("negmax", [P, JT, HEADS])
        self.negpad = sb("negpad", [P, JT, HEADS, 32])
        self.expneg = sb("expneg", [P, JT, HEADS])
        self.e = sb("e", [P, 2, JT, 4, S])
        self.num = sb("num", [P, JT * HEADS, VW])
        self.rec = sb("rec", [P, JT * HEADS])
        self.att = sb("att", [P, TILES, D])
        self.att_t = sb("att_t", [P, GROUP])
        self.sems = c.attention_sems
        b = c.bank
        self.p1 = [b[0], b[1]]
        self.p2 = [c.psum[:, 1024:2048].rearrange("p (t q) -> p t q", t=HT), b[4].rearrange("p (t q) -> p t q", t=HT)]
        self.misc, self.o = b[5], b[6]
        self.both = c.psum[:, 3072:4096]

    def keys(self, j):
        return S if (j == 1) == self.causal else P

    def queries(self, ch):
        if ch == 0:
            return 0, S
        return (P, S) if self.causal else (0, P)

    def pass1(self, pe, n, s, units):
        c, nc, W = self.c, self.c.nc, self.masks
        for at in units:
            j, g, half = at // 8, at % 8 // 2, at % 2
            kw = self.keys(j)
            u = s * P1 + at
            if u >= 2:
                pe.wait_ge(self.sems.s_mx, n * (SEQ_G * P1) + (u - 1))
            ps = self.p1[u % 2].rearrange("p (g k) -> p g k", g=2)[:, :, 0:kw]
            nc.tensor.matmul(ps, c.ident_bf[:], W["negq"][:, j, :, 0:kw], start=True, stop=True)
            for tt in range(2):
                T = 2 * half + tt
                last = nc.tensor.matmul(ps[:, tt], self.q[:, T, s * S + j * P:s * S + (j + 1) * P],
                                        self.k[:, T, g, s * S:s * S + kw], start=False, stop=True, skip_group_check=True)
            last.then_inc(self.sems.s_p1, 1)

    def turn_max(self, pe, n, s):
        c, nc = self.c, self.c.nc
        pe.wait_ge(self.sems.s_negpad, n * SEQ_G + (s + 1))
        for half in range(2):
            if half:
                pe.wait_ge(self.sems.s_qaug, n * (2 * SEQ_G) + (2 * s + 1))
            for tt in range(2):
                T = 2 * half + tt
                for j in range(JT):
                    at = tt * S + j * P
                    last = nc.tensor.transpose(self.misc[:, at:at + P], self.negpad[:, j, 4 * T:4 * T + 4, :].rearrange("p g r -> p (g r)"), c.ident)
            last.then_inc(self.sems.s_nm, 1)

    def scores_t(self, pe, n, s, g):
        c, nc, W = self.c, self.c.nc, self.masks
        for ch in range(JT):
            a, b = self.queries(ch)
            u = s * P2 + g * 2 + ch
            if u >= 2:
                pe.wait_ge(self.sems.s_e, n * (SEQ_G * P2) + (u - 1))
            ps = self.p2[ch]
            if ch == 1:
                nc.tensor.matmul(ps, c.ident_bf[:], W["negk"][:, 1, 0:1, a:b].broadcast_to([P, HT, P]), start=True, stop=True)
            for half in range(2 if ch == 0 else 0):
                nc.tensor.matmul(ps[:, 2 * half:2 * half + 2], c.ident_bf[:], W["negk"][:, ch, :, a:b], start=True, stop=True)
            for T in range(HT):
                last = nc.tensor.matmul(ps[:, T], self.k[:, T, g, s * S + ch * P:s * S + (ch + 1) * P],
                                        self.q[:, T, s * S + a:s * S + b], start=False, stop=True,
                                        skip_group_check=True)
            last.then_inc(self.sems.s_p2, 1)

    def values(self, pe, n, s, g):
        nc = self.c.nc
        pe.wait_ge(self.sems.s_e, n * (SEQ_G * P2) + (s * P2 + 2 * g + 2))
        o = self.both.rearrange("p (t q) -> p t q", t=HT)[32 * g:32 * g + 32]
        for T in range(HT):
            for ch in range(JT):
                a, b = self.queries(ch)
                last = nc.tensor.matmul(o[:, T, a:b], self.v[:, s * JT + ch, 4 * T + g], self.e[:, g % 2, ch, T, a:b],
                                        start=(ch == 0), stop=True, skip_group_check=(ch > 0))
        last.then_inc(self.sems.s_pv, 1)

    def turn_back(self, pe, n, s):
        pe.wait_ge(self.sems.s_ot, n * SEQ_G + (s + 1))
        for j in range(JT):
            for T in range(HT):
                at = (j * HT + T) * P
                last = self.c.nc.tensor.transpose(self.both[:, at:at + P], self.o_t[:, T, j * P:(j + 1) * P], self.c.ident)
        last.then_inc(self.sems.s_o, 1)

    def masked_sum(self, pe, n, s):
        nc = self.c.nc
        u = self.misc[:, 0:JT * HEADS * VW].rearrange("p (j h v) -> p j h v", j=JT, v=VW)
        for j in range(JT):
            for ch in range(JT):
                last = nc.tensor.matmul(u[:, j], self.masks["zero"][:, ch, j * P:(j + 1) * P],
                                        self.v[:, s * JT + ch, :, 0:VW], start=(ch == 0), stop=(ch == 1))
        last.then_inc(self.sems.s_u, 1)

    def core_tensor(self, pe, n):
        nc, c = self.c.nc, self.c
        pe.wait_ge(self.sems.s_qev, n * HT + HT)
        pe.wait_ge(self.sems.s_kev, n * HT + HT)
        pe.wait_ge(self.sems.s_v, n + 1)
        self.pass1(pe, n, 0, range(P1))
        for s in range(SEQ_G):
            if s:
                pe.wait_ge(self.sems.s_num, n * SEQ_G + s)
            self.turn_max(pe, n, s)
            pe.wait_ge(self.sems.s_qaug, n * (2 * SEQ_G) + (2 * s + 2))
            if not self.causal:
                self.masked_sum(pe, n, s)
            for g in range(4):
                self.scores_t(pe, n, s, g)
                if s + 1 < SEQ_G:
                    self.pass1(pe, n, s + 1, range(4 * g, 4 * g + 4))
                if g >= 1:
                    self.values(pe, n, s, g - 1)
            self.values(pe, n, s, 3)
            self.turn_back(pe, n, s)
        pe.wait_ge(self.sems.s_att, n * SEQ_G + SEQ_G)
        for t in range(TILES):
            last = nc.tensor.transpose(self.misc[:, t * P:(t + 1) * P], self.att[:, t, :], c.ident)
        last.then_inc(self.sems.s_att_t, 1)

    def maxima(self, dve, n, s):
        nc = self.c.nc
        for at in range(P1):
            j, g, half = at // 8, at % 8 // 2, at % 2
            kw = self.keys(j)
            u = s * P1 + at
            dve.wait_ge(self.sems.s_p1, n * (SEQ_G * P1) + (u + 1))
            ps = self.p1[u % 2].rearrange("p (g k) -> p g k", g=2)[:, :, 0:kw]
            out = self.mx[:, j].rearrange("p (t g) -> p t g", g=4)[:, 2 * half:2 * half + 2, g]
            nc.vector.tensor_reduce(out, ps, AX_X, ALU.max).then_inc(self.sems.s_mx, 1)

    def augment(self, dve, n, s):
        nc = self.c.nc
        dve.wait_ge(self.sems.s_mx, n * (SEQ_G * P1) + (s + 1) * P1)
        for j in range(JT):
            last = nc.vector.tensor_scalar(self.negmax[:, j], self.mx[:, j], self.masks["floor"][:, j:j + 1], -1.0,
                                           ALU.max, ALU.mult)
        last.then_inc(self.sems.s_negmax, 1)
        dve.wait_ge(self.sems.s_negmax, n * SEQ_G + (s + 1))
        nc.vector.tensor_copy(self.negpad[:].rearrange("p j h r -> p (j h) r")[:, :, 0:1],
                              self.negmax[:].rearrange("p j (h r) -> p (j h) r", r=1)).then_inc(self.sems.s_negpad, 1)
        for half in range(2):
            dve.wait_ge(self.sems.s_nm, n * (2 * SEQ_G) + (2 * s + half + 1))
            q = self.q[:, 2 * half:2 * half + 2, s * S:(s + 1) * S]
            nc.vector.tensor_tensor(q, self.misc.rearrange("p (t q) -> p t q", t=2), q, ALU.add).then_inc(self.sems.s_qaug, 1)

    def sums(self, dve, n, s):
        nc = self.c.nc
        o = self.both.rearrange("p (h v) -> p h v", v=32)[:, :, 0:VW]
        u = self.misc[:, 0:JT * HEADS * VW].rearrange("p (h v) -> p h v", v=VW)
        num = self.num[:]
        if not self.causal:
            dve.wait_ge(self.sems.s_u, n * SEQ_G + (s + 1))
            dve.wait_ge(self.sems.s_expneg, n * SEQ_G + (s + 1))
            e = self.expneg[:].rearrange("p j h -> p (j h)").unsqueeze(2).broadcast_to([P, JT * HEADS, VW])
            nc.vector.tensor_tensor(num, u, e, ALU.mult).then_inc(self.sems.s_num0, 1)
            dve.wait_ge(self.sems.s_o, n * SEQ_G + (s + 1))
            dve.wait_ge(self.sems.s_num0, n * SEQ_G + (s + 1))
            nc.vector.tensor_tensor(num, o, num, ALU.add).then_inc(self.sems.s_num, 1)
        else:
            dve.wait_ge(self.sems.s_o, n * SEQ_G + (s + 1))
            nc.vector.tensor_copy(num, o).then_inc(self.sems.s_num, 1)

    def core_vector(self, dve, n):
        self.maxima(dve, n, 0)
        for s in range(SEQ_G):
            self.augment(dve, n, s)
            if s + 1 < SEQ_G:
                self.maxima(dve, n, s + 1)
            self.sums(dve, n, s)
            self.normalise(dve, n, s)

    def normalise(self, dve, n, s, eps=None):
        nc, num = self.c.nc, self.num[:]
        dve.wait_ge(self.sems.s_num, n * SEQ_G + (s + 1))
        nc.vector.reciprocal(self.rec[:].unsqueeze(2), num[:, :, 0:1]).then_inc(self.sems.s_rec, 1)
        dve.wait_ge(self.sems.s_rec, n * SEQ_G + (s + 1))
        out = self.att[:, s * JT:(s + 1) * JT, :].rearrange("p j (h d) -> p (j h) d", h=HEADS)
        nc.vector.tensor_tensor(out, num[:, :, 1:VW], self.rec[:].unsqueeze(2).broadcast_to([P, JT * HEADS, HD]),
                                ALU.mult).then_inc(self.sems.s_att, 1)

    def core_scalar(self, act, n):
        nc = self.c.nc
        for s in range(SEQ_G):
            if not self.causal:
                act.wait_ge(self.sems.s_negmax, n * SEQ_G + (s + 1))
                nc.scalar.activation(self.expneg[:], self.negmax[:], ACT.Exp).then_inc(self.sems.s_expneg, 1)
            for g in range(4):
                if s * HT + g >= 2:
                    act.wait_ge(self.sems.s_pv, n * (SEQ_G * HT) + (s * HT + g - 1))
                for ch in range(JT):
                    a, b = self.queries(ch)
                    u = s * P2 + g * 2 + ch
                    act.wait_ge(self.sems.s_p2, n * (SEQ_G * P2) + (u + 1))
                    nc.scalar.activation(self.e[:, g % 2, ch, :, a:b], self.p2[ch], ACT.Exp).then_inc(self.sems.s_e, 1)
            act.wait_ge(self.sems.s_pv, n * (SEQ_G * HT) + (s + 1) * HT)
            nc.scalar.activation(self.o_t[:].rearrange("p t q -> p (t q)"), self.both, ACT.Copy).then_inc(self.sems.s_ot, 1)

    def rows_tensor(self, pe, n, wo, bias=None):
        nc, c = self.c.nc, self.c
        pe.wait_ge(self.sems.s_att_tm, n + 1)
        for t in range(TILES):
            sl = slice(t * P, (t + 1) * P)
            nc.tensor.matmul(self.o[:, sl], self.att_t[:, sl], wo, start=True, stop=False)
            if bias is not None:
                nc.tensor.matmul(self.o[:, sl], c.ones[0:1, 0:P], bias, start=False, stop=False)
            last = nc.tensor.matmul(self.o[:, sl], c.cur[:, sl], c.ident, start=False, stop=True)
        last.then_inc(self.sems.s_rows, 1)

    def rows_scalar(self, act, n):
        act.wait_ge(self.sems.s_att_t, n + 1)
        self.c.nc.scalar.activation(self.att_t[:], self.misc, ACT.Copy).then_inc(self.sems.s_att_tm, 1)


def init_attention(c, A, pool, s_init, s_zero):
    c.nc.gpsimd.memset(A.v[:], 0.0).then_inc(s_zero, 1)
    pool.wait_ge(s_zero, 1)
    c.nc.gpsimd.memset(A.v[:].rearrange("p t h v -> p (t h) v")[:, :, 0:1], 1.0)
    c.nc.gpsimd.memset(A.negpad[:], 0.0).then_inc(s_init, 1)



def rope_attention(c, base):
    nc = c.nc
    with ExitStack() as ctx:
        def sem(n): return c.sem("rope_" + n)
        W = load_stage(c, ctx, "s7")
        A = Attention(c, ctx, "rope_", causal=True)
        neg = ctx.enter_context(nc.sbuf_tensor("rope_neg", [P, 2, JT, 2, S], BF16))
        A.masks = {"negq": neg[:, 0], "negk": neg[:, 1], "floor": W["floor"]}
        n0 = c.attended
        c.attended += GROUPS
        t1 = ctx.enter_context(nc.sbuf_tensor("rope_t1", [P, GROUP], F32))
        t2 = ctx.enter_context(nc.sbuf_tensor("rope_t2", [P, GROUP], F32))
        t3 = ctx.enter_context(nc.sbuf_tensor("rope_t3", [P, GROUP], F32))
        s_key = sem("key_ready")
        s_init, s_straight, s_swapped = sem("init"), sem("straight_scaled"), sem("swapped_scaled")
        block = ctx.enter_context(nc.Block())

        @block.sync
        def _(sp):
            W.start(sp)

        @block.gpsimd
        def _(pool):
            init_attention(c, A, pool, s_init, sem("values_zeroed"))
            with pool.Fori(0, GROUPS) as i:
                fetch_group(c, pool, i + base, i)
                norm_pool(c, pool, i + base)

        @block.tensor
        def _(pe):
            W.wait(pe)
            pe.wait_ge(s_init, 2)
            with pe.Fori(0, GROUPS) as i:
                pe.wait_ge(c.s_cur, i + (base + 1))
                for w in range(2):
                    for T in range(HT):
                        m = w * HT + T
                        if m >= 1:
                            pe.wait_ge((A.sems.s_qev, A.sems.s_kev)[(m - 1) // HT], (i + n0) * HT + ((m - 1) % HT + 1))
                        wt = W["wqk"].rearrange("p (w x t n) -> p w x t n", w=2, x=2, t=HT)
                        nc.tensor.matmul(A.o, wt[:, w, 0, T], c.cur[:], start=True, stop=True)
                        nc.tensor.matmul(A.misc, wt[:, w, 1, T], c.cur[:], start=True, stop=True).then_inc(A.sems.s_proj, 1)
                pe.wait_ge(A.sems.s_kev, (i + n0) * HT + HT)
                for t in range(TILES):
                    last = nc.tensor.matmul(A.o[:, t * P:(t + 1) * P], c.cur[:, t * P:(t + 1) * P], W["wv"], start=True, stop=True)
                last.then_inc(A.sems.s_vp, 1)
                A.core_tensor(pe, i + n0)
                A.rows_tensor(pe, i + n0, W["wo"])
                norm_tensor(c, pe, i + base)

        @block.vector
        def _(dve):
            W.wait(dve)
            nc.vector.tensor_copy(neg[:].rearrange("p a j d s -> p (a j d s)"), W["neg"]).then_inc(s_init, 1)
            dve.wait_ge(s_init, 2)
            rows = A.o.rearrange("p (t d) -> p t d", t=TILES)
            with dve.Fori(0, GROUPS) as i:
                for w in range(2):
                    for T in range(HT):
                        m = w * HT + T
                        dve.wait_ge(A.sems.s_proj, (i + n0) * (2 * HT) + (m + 1))
                        rot = W["rot"].rearrange("p (w x n) -> p w x n", w=2, x=2)
                        nc.vector.tensor_tensor(t1[:], A.o, rot[:, w, 0], ALU.mult).then_inc(s_straight, 1)
                        nc.vector.tensor_tensor(t2[:], A.misc, rot[:, w, 1], ALU.mult).then_inc(s_swapped, 1)
                        dve.wait_ge(s_straight, i * (2 * HT) + (m + 1))
                        dve.wait_ge(s_swapped, i * (2 * HT) + (m + 1))
                        if w == 0:
                            nc.vector.tensor_tensor(A.q[:, T], t1[:], t2[:], ALU.add).then_inc(A.sems.s_qev, 1)
                        else:
                            nc.vector.scalar_tensor_tensor(out=t3[:], in0=t1[:], scalar=W["row"][:, 0:1], in1=t2[:],
                                                           op0=ALU.add, op1=ALU.add).then_inc(s_key, 1)
                            dve.wait_ge(s_key, i * HT + (T + 1))
                            for g in range(4):
                                last = nc.vector.tensor_scalar(A.k[:, T, g], t3[:], W["heads"][:, g:g + 1], None, ALU.mult)
                            last.then_inc(A.sems.s_kev, 1)
                        dve.wait_ge((A.sems.s_qev, A.sems.s_kev)[w], (i + n0) * HT + (T + 1))
                dve.wait_ge(A.sems.s_vp, i + (n0 + 1))
                nc.vector.tensor_copy(A.v[:].rearrange("p t h v -> p (t h) v")[:, :, 1:VW],
                                      A.o.rearrange("p (h d) -> p h d", d=HD)).then_inc(A.sems.s_v, 1)
                A.core_vector(dve, i + n0)
                norm_vector(c, dve, i + base, rows, (A.sems.s_rows, i + (n0 + 1)))

        @block.scalar
        def _(act):
            with act.Fori(0, GROUPS) as i:
                A.core_scalar(act, i + n0)
                A.rows_scalar(act, i + n0)
                norm_scalar(c, act, i + base, ds(i * GROUP, GROUP))
    return base + GROUPS


LAYERS = 6


def encoder(c, base):
    nc = c.nc
    with ExitStack() as ctx:
        def sem(n): return c.sem("enc_" + n)
        def sb(n, shape, dt=F32): return ctx.enter_context(nc.sbuf_tensor("enc_" + n, shape, dt))
        W = load_stage(c, ctx, "s1")
        L = load_stage(c, ctx, "layer0")
        A = Attention(c, ctx, "enc_", causal=False)
        neg = sb("neg", [P, 2, JT, 2, S], BF16)
        x0 = sb("x0", [P, TOKENS])
        hidden = sb("hidden", [P, 4, GROUP])
        A.masks = {"negq": neg[:, 0], "negk": neg[:, 1], "floor": W["floor"],
                   "zero": W["zero"].rearrange("p (c q) -> p c q", c=JT)}
        s_init, s_x0, s_pos = sem("init"), sem("x0_loaded"), sem("positions_added")
        s_h, s_g, s_rows2, s_rows3 = sem("hidden_ready"), sem("gelu_ready"), sem("ffn_rows_ready"), sem("last_rows_ready")
        PER = 2 * GROUPS
        proj = lambda T, w: c.bank[2 + (2 * T + w) % 4]
        last_base = base + LAYERS * PER
        c.attended += LAYERS * GROUPS
        block = ctx.enter_context(nc.Block())

        @block.sync
        def _(sp):
            W.start(sp)
            sp.dma_start(x0[:], c.x_t).then_inc(s_x0, 16)
            with sp.Fori(0, LAYERS) as layer:
                sp.wait_ge(c.s_done, layer * PER + (base + 1))
                sp.dma_start(L.sb[:], c.layer_params[ds(layer, 1)].rearrange("l p w -> p (l w)")).then_inc(L.sem, 16)

        @block.gpsimd
        def _(pool):
            init_attention(c, A, pool, s_init, sem("values_zeroed"))
            pool.wait_ge(s_pos, 1)
            with pool.Fori(0, LAYERS * PER) as m:
                norm_pool(c, pool, m + base)
            with pool.Fori(0, GROUPS) as i:
                fetch_group(c, pool, i + last_base, i)
                norm_pool(c, pool, i + last_base)
            pool.wait_ge(s_x0, 16)
            with pool.Fori(0, GROUPS) as i:
                n = i + (last_base + GROUPS)
                pool.wait_ge(c.s_done, n + 1)
                nc.gpsimd.tensor_tensor(c.cur[:], c.H[:, ds(i * GROUP, GROUP)], x0[:, ds(i * GROUP, GROUP)], ALU.add)\
                    .then_inc(c.s_cur, 1)
                norm_pool(c, pool, n)

        @block.tensor
        def _(pe):
            W.wait(pe)
            pe.wait_ge(s_init, 2)
            with pe.Fori(0, LAYERS) as layer:
                def project(i, between=None):
                    m, n = layer * GROUPS + i, layer * PER + i + base
                    pe.wait_ge(L.sem, layer * 16 + 16)
                    pe.wait_ge(c.s_cur, n + 1)
                    for T in range(HT):
                        for w, (name, moved) in enumerate((("wq", A.sems.s_qev), ("wk", A.sems.s_kev))):
                            if T >= 2:
                                pe.wait_ge(moved, m * HT + (T - 1))
                            nc.tensor.matmul(proj(T, w), L[name][:, T * P:(T + 1) * P], c.cur[:], start=True, stop=True).then_inc(A.sems.s_proj, 1)
                        if T == 0 and between:
                            between()
                    for t in range(TILES):
                        sl = slice(t * P, (t + 1) * P)
                        nc.tensor.matmul(c.bank[1][:, sl], c.cur[:, sl], L["wv"], start=True, stop=False)
                        last = nc.tensor.matmul(c.bank[1][:, sl], c.ones[0:1, 0:P], L["bv"][0:1], start=False, stop=True)
                    last.then_inc(A.sems.s_vp, 1)

                def attend(i):
                    m, n = layer * GROUPS + i, layer * PER + i + base
                    pe.wait_ge(c.s_done, n + 1)
                    A.core_tensor(pe, m)
                    A.rows_tensor(pe, m, L["wo"], L["bo"][0:1])

                def attend_and_go_on(i):
                    attend(i)
                    project(i + 1, lambda: norm_tensor(c, pe, layer * PER + i + base))

                def attend_last(i):
                    attend(i)
                    norm_tensor(c, pe, layer * PER + i + base)

                over_groups(pe, project, attend_and_go_on, attend_last)

                def up(i):
                    n = layer * PER + i + (base + GROUPS)
                    pe.wait_ge(c.s_cur, n + 1)
                    for f in range(4):
                        nc.tensor.matmul(c.bank[1 + f], L["w1"][:, f * P:(f + 1) * P], c.cur[:], start=True, stop=True).then_inc(s_h, 1)

                def down(i):
                    m = layer * GROUPS + i
                    for t in range(TILES):
                        sl = slice(t * P, (t + 1) * P)
                        nc.tensor.matmul(A.o[:, sl], c.cur[:, sl], c.ident, start=True, stop=False)
                        nc.tensor.matmul(A.o[:, sl], c.ones[0:1, 0:P], L["b2"][0:1], start=False, stop=False)
                        for f in range(4):
                            if t == 0:
                                pe.wait_ge(s_g, m * 4 + (f + 1))
                            last = nc.tensor.matmul(A.o[:, sl], hidden[:, f, sl], L["w2"][:, f * P:(f + 1) * P], start=False, stop=(f == 3))
                    last.then_inc(s_rows2, 1)

                def down_and_go_on(i):
                    down(i)
                    up(i + 1)
                    norm_tensor(c, pe, layer * PER + i + (base + GROUPS))

                def down_last(i):
                    down(i)
                    norm_tensor(c, pe, layer * PER + i + (base + GROUPS))

                over_groups(pe, up, down_and_go_on, down_last)
            with pe.Fori(0, 2 * GROUPS) as i:
                n = i + last_base
                pe.wait_ge(c.s_cur, n + 1)
                for t in range(TILES):
                    last = nc.tensor.transpose(A.o[:, t * P:(t + 1) * P], c.cur[:, t * P:(t + 1) * P], c.ident)
                last.then_inc(s_rows3, 1)
                norm_tensor(c, pe, n)

        @block.vector
        def _(dve):
            W.wait(dve)
            nc.vector.tensor_copy(neg[:].rearrange("p a j d s -> p (a j d s)"), W["neg"]).then_inc(s_init, 1)
            h = c.H[:].rearrange("p (g s) -> p g s", s=S)
            nc.vector.tensor_tensor(h, h, W["pos"].unsqueeze(1).broadcast_to([P, SEQS, S]), ALU.add).then_inc(s_pos, 1)
            dve.wait_ge(s_init, 2)
            dve.wait_ge(s_pos, 1)
            rows = A.o.rearrange("p (t d) -> p t d", t=TILES)
            with dve.Fori(0, LAYERS) as layer:
                def move(i):
                    m = layer * GROUPS + i
                    for T in range(HT):
                        dve.wait_ge(A.sems.s_proj, m * (2 * HT) + (2 * T + 1))
                        nc.vector.tensor_scalar(A.q[:, T], proj(T, 0), L["bq"][:, T:T + 1], HD ** -0.5, ALU.add, ALU.mult).then_inc(A.sems.s_qev, 1)
                    dve.wait_ge(A.sems.s_vp, m + 1)
                    nc.vector.tensor_copy(A.v[:].rearrange("p t h v -> p (t h) v")[:, :, 1:VW],
                                          c.bank[1].rearrange("p (h d) -> p h d", d=HD)).then_inc(A.sems.s_v, 1)

                def first(i):
                    dve.wait_ge(L.sem, layer * 16 + 16)
                    dve.wait_ge(c.s_done, layer * PER + (base + 1))
                    fetch_ahead(c, dve, i)
                    move(i)

                def attend(i):
                    m, n = layer * GROUPS + i, layer * PER + i + base
                    dve.wait_ge(A.sems.s_qev, m * HT + HT)
                    A.core_vector(dve, m)
                    norm_statistics(c, dve, n, rows, (A.sems.s_rows, m + 1))

                def attend_and_go_on(i):
                    attend(i)
                    fetch_ahead(c, dve, i + 1)
                    norm_apply(c, dve, layer * PER + i + base, rows)
                    move(i + 1)

                def attend_last(i):
                    attend(i)
                    norm_apply(c, dve, layer * PER + i + base, rows)

                over_groups(dve, first, attend_and_go_on, attend_last)

                def first_ffn(i):
                    dve.wait_ge(c.s_done, layer * PER + (base + GROUPS + 1))
                    fetch_ahead(c, dve, i)

                def ffn_and_go_on(i):
                    n = layer * PER + i + (base + GROUPS)
                    norm_statistics(c, dve, n, rows, (s_rows2, layer * GROUPS + i + 1))
                    fetch_ahead(c, dve, i + 1)
                    norm_apply(c, dve, n, rows)

                def ffn_last(i):
                    norm_vector(c, dve, layer * PER + i + (base + GROUPS), rows, (s_rows2, layer * GROUPS + i + 1))

                over_groups(dve, first_ffn, ffn_and_go_on, ffn_last)
            with dve.Fori(0, 2 * GROUPS) as i:
                norm_vector(c, dve, i + last_base, rows, (s_rows3, i + 1))

        @block.scalar
        def _(act):
            with act.Fori(0, LAYERS) as layer:
                def normed(i, half):
                    g, b = (L["g1"], L["be1"]) if half == 0 else (L["g2"], L["be2"])
                    norm_scalar(c, act, layer * PER + i + (base + half * GROUPS), ds(i * GROUP, GROUP), g, b)

                def move(i, between=None):
                    m = layer * GROUPS + i
                    act.wait_ge(L.sem, layer * 16 + 16)
                    for T in range(HT):
                        act.wait_ge(A.sems.s_proj, m * (2 * HT) + (2 * T + 2))
                        for g in range(4):
                            last = nc.scalar.activation(A.k[:, T, g], proj(T, 1), ACT.Identity, bias=L["bk"][:, 4 * T + g:4 * T + g + 1],
                                                        scale=W["heads"][:, g:g + 1])
                        last.then_inc(A.sems.s_kev, 1)
                        if T == 0 and between:
                            between()

                def attend(i):
                    m = layer * GROUPS + i
                    A.core_scalar(act, m)
                    A.rows_scalar(act, m)

                def attend_and_go_on(i):
                    attend(i)
                    move(i + 1, lambda: normed(i, 0))

                def attend_last(i):
                    attend(i)
                    normed(i, 0)

                over_groups(act, move, attend_and_go_on, attend_last)

                def gelu(i):
                    m = layer * GROUPS + i
                    for f in range(4):
                        act.wait_ge(s_h, m * 4 + (f + 1))
                        nc.scalar.activation(hidden[:, f], c.bank[1 + f], ACT.Gelu, bias=L["b1"][:, f:f + 1]).then_inc(s_g, 1)

                def gelu_and_normed(i):
                    gelu(i + 1)
                    normed(i, 1)

                over_groups(act, gelu, gelu_and_normed, lambda i: normed(i, 1))
            with act.Fori(0, GROUPS) as i:
                norm_scalar(c, act, i + last_base, ds(i * GROUP, GROUP), W["gf"], W["bf"])
            with act.Fori(0, GROUPS) as i:
                norm_scalar(c, act, i + (last_base + GROUPS), ds(i * GROUP, GROUP))
    return last_base + 2 * GROUPS



EXPERTS = 8
FF = 4 * D
FC = FF // P


def experts(c, base):
    nc = c.nc
    with ExitStack() as ctx:
        def sem(n): return c.sem("moe_" + n)
        def sb(n, shape, dt=F32): return ctx.enter_context(nc.sbuf_tensor("moe_" + n, shape, dt))
        W = load_stage(c, ctx, "s2")
        logits = sb("logits", [P, TILES, EXPERTS])
        above = sb("above", [P, TILES, EXPERTS, EXPERTS])
        equal = sb("equal", [P, TILES, EXPERTS, EXPERTS])
        rank = sb("rank", [P, TILES, EXPERTS])
        top = sb("top", [P, TILES])
        shifted = sb("shifted", [P, TILES, EXPERTS])
        weight = sb("weight", [P, TILES, EXPERTS])
        total = sb("total", [P, TILES])
        gates = sb("gates", [P, TILES, EXPERTS])
        act_h = sb("act_h", [P, 2, FC, GROUP])
        acc = sb("acc", [P, TILES, D])
        s_logit, s_h, s_silu, s_down, s_acc = sem("logits_ready"), sem("hidden_ready"), sem("silu_ready"), sem("down_ready"), sem("added")
        s_gate = sem("gate_step")
        s_exp = sem("gate_exp_ready")
        GATE = 10
        E1 = EXPERTS + 1
        block = ctx.enter_context(nc.Block())

        @block.sync
        def _(sp):
            W.start(sp)

        @block.gpsimd
        def _(pool):
            with pool.Fori(0, GROUPS) as i:
                fetch_group(c, pool, i + base, i)
                norm_pool(c, pool, i + base)

        @block.tensor
        def _(pe):
            W.wait(pe)
            with pe.Fori(0, GROUPS) as i:
                pe.wait_ge(c.s_cur, i + (base + 1))
                for t in range(TILES):
                    last = nc.tensor.matmul(c.bank[7][:, t * EXPERTS:(t + 1) * EXPERTS], c.cur[:, t * P:(t + 1) * P], W["gate"], start=True, stop=True)
                last.then_inc(s_logit, 1)

                def up(e):
                    for f in range(FC):
                        m = e * FC + f
                        if m >= 4:
                            pe.wait_ge(s_silu, i * (E1 * FC) + (m - 3))
                        at = (e * FC + f) * P
                        nc.tensor.matmul(c.bank[1 + f], W["w1"][:, at:at + P], c.cur[:], start=True, stop=True).then_inc(s_h, 1)

                def down(e):
                    pe.wait_ge(s_silu, i * (E1 * FC) + (e + 1) * FC)
                    if e >= 2:
                        pe.wait_ge(s_acc, i * E1 + (e - 1))
                    b = c.bank[5 + e % 2]
                    for t in range(TILES):
                        sl = slice(t * P, (t + 1) * P)
                        if e == 0:
                            nc.tensor.matmul(b[:, sl], c.cur[:, sl], c.ident, start=True, stop=False)
                        for f in range(FC):
                            at = (e * FC + f) * P
                            last = nc.tensor.matmul(b[:, sl], act_h[:, e % 2, f, sl], W["w2"][:, at:at + P],
                                                    start=(f == 0 and e > 0), stop=(f == FC - 1))
                    last.then_inc(s_down, 1)

                up(0)
                for e in range(1, E1):
                    up(e)
                    down(e - 1)
                down(E1 - 1)
                norm_tensor(c, pe, i + base)

        @block.vector
        def _(dve):
            W.wait(dve)
            with dve.Fori(0, GROUPS) as i:
                def step(k, ins):
                    ins.then_inc(s_gate, 1)
                    dve.wait_ge(s_gate, i * GATE + k)
                dve.wait_ge(s_logit, i + 1)
                bank = c.bank[7][:, 0:TILES * EXPERTS].rearrange("p (t e) -> p t e", t=TILES)
                step(1, nc.vector.tensor_copy(logits[:], bank))
                full = [P, TILES, EXPERTS, EXPERTS]
                mine = logits[:].unsqueeze(3).broadcast_to(full)
                other = logits[:].unsqueeze(2).broadcast_to(full)
                nc.vector.tensor_tensor(above[:], other, mine, ALU.is_gt)
                step(2, nc.vector.tensor_tensor(equal[:], other, mine, ALU.is_equal))
                before = W["before"].rearrange("p (a b) -> p a b", a=EXPERTS).unsqueeze(1).broadcast_to(full)
                step(3, nc.vector.tensor_tensor(equal[:], equal[:], before, ALU.mult))
                step(4, nc.vector.tensor_tensor(above[:], above[:], equal[:], ALU.add))
                nc.vector.tensor_reduce(rank[:], above[:], AX_X, ALU.add)
                step(5, nc.vector.tensor_reduce(top[:], logits[:], AX_X, ALU.max))
                three = [P, TILES, EXPERTS]
                step(6, nc.vector.tensor_tensor(shifted[:], logits[:], top[:].unsqueeze(2).broadcast_to(three), ALU.subtract))
                dve.wait_ge(s_exp, i + 1)
                step(7, nc.vector.scalar_tensor_tensor(out=weight[:], in0=rank[:], scalar=1.5, in1=weight[:], op0=ALU.is_lt, op1=ALU.mult))
                step(8, nc.vector.tensor_reduce(total[:], weight[:], AX_X, ALU.add))
                step(9, nc.vector.reciprocal(total[:], total[:]))
                step(10, nc.vector.tensor_tensor(gates[:], weight[:], total[:].unsqueeze(2).broadcast_to(three), ALU.mult))
                for e in range(E1):
                    dve.wait_ge(s_down, i * E1 + (e + 1))
                    b = c.bank[5 + e % 2].rearrange("p (t d) -> p t d", t=TILES)
                    if e == 0:
                        nc.vector.tensor_copy(acc[:], b).then_inc(s_acc, 1)
                    else:
                        for t in range(TILES):
                            if t == 0:
                                dve.wait_ge(s_acc, i * E1 + e)
                            last = nc.vector.scalar_tensor_tensor(out=acc[:, t], in0=b[:, t], scalar=gates[:, t, e - 1:e],
                                                                  in1=acc[:, t], op0=ALU.mult, op1=ALU.add)
                        last.then_inc(s_acc, 1)
                norm_vector(c, dve, i + base, acc, (s_acc, i * E1 + E1))

        @block.scalar
        def _(act):
            with act.Fori(0, GROUPS) as i:
                act.wait_ge(s_gate, i * GATE + 6)
                nc.scalar.activation(weight[:], shifted[:], ACT.Exp).then_inc(s_exp, 1)
                for e in range(E1):
                    if e >= 2:
                        act.wait_ge(s_down, i * E1 + (e - 1))
                    for f in range(FC):
                        act.wait_ge(s_h, i * (E1 * FC) + (e * FC + f + 1))
                        nc.scalar.activation(act_h[:, e % 2, f], c.bank[1 + f], ACT.Silu).then_inc(s_silu, 1)
                norm_scalar(c, act, i + base, ds(i * GROUP, GROUP))
    return base + GROUPS


BLK = 16
FF4 = 352
FF4P = 384
XB, HB = D // BLK, FF4P // BLK
QSTEPS = 11


class Quantiser:

    def __init__(self, c, ctx, tag, blocks):
        nc = c.nc
        def sb(n, shape, dt=F32): return ctx.enter_context(nc.sbuf_tensor(tag + n, shape, dt))
        self.nc, self.blocks = nc, blocks
        self.xn, self.low, self.high = sb("xn", [P, blocks, BLK]), sb("low", [P, blocks, BLK]), sb("high", [P, blocks, BLK])
        self.scale, self.inv, self.half = sb("scale", [P, blocks]), sb("inv", [P, blocks]), sb("half", [P, blocks])
        self.sem = c.sem(tag + "step")

    def run(self, dve, n, x, out, done):
        nc = self.nc
        B = x.shape[1]
        xn, low, high = self.xn[:, 0:B], self.low[:, 0:B], self.high[:, 0:B]
        scale, inv, half = self.scale[:, 0:B], self.inv[:, 0:B], self.half[:, 0:B]
        bc = lambda a: a.unsqueeze(2).broadcast_to([P, B, BLK])

        def step(k, ins):
            ins.then_inc(self.sem, 1)
            dve.wait_ge(self.sem, n * QSTEPS + k)

        step(1, nc.vector.tensor_reduce(scale, x, AX_X, ALU.max, apply_absolute_value=True))
        step(2, nc.vector.tensor_scalar(scale, scale, 1.0 / 6.0, 1e-12, ALU.mult, ALU.max))
        nc.vector.reciprocal(inv, scale)
        step(3, nc.vector.tensor_scalar(half, scale, 0.5, None, ALU.mult))
        step(4, nc.vector.tensor_tensor(xn, x, bc(inv), ALU.mult))
        step(5, nc.vector.tensor_scalar(xn.bitcast(U32), xn.bitcast(U32), 0x7FFFFFFF, None, ALU.bitwise_and))
        nc.vector.tensor_scalar(high, xn, 5.0, 2.0, ALU.is_gt, ALU.mult)
        step(6, nc.vector.tensor_scalar(low, xn, 0.25, None, ALU.is_gt))
        for k, (lo, hi) in enumerate(((0.75, 2.5), (1.25, 3.5))):
            nc.vector.scalar_tensor_tensor(out=low, in0=xn, scalar=lo, in1=low, op0=ALU.is_gt, op1=ALU.add)
            step(7 + k, nc.vector.scalar_tensor_tensor(out=high, in0=xn, scalar=hi, in1=high, op0=ALU.is_gt, op1=ALU.add))
        step(9, nc.vector.scalar_tensor_tensor(out=low, in0=xn, scalar=1.75, in1=low, op0=ALU.is_gt, op1=ALU.add))
        step(10, nc.vector.scalar_tensor_tensor(out=high, in0=high, scalar=2.0, in1=low, op0=ALU.mult, op1=ALU.add))
        step(11, nc.vector.tensor_tensor(low, high, bc(half), ALU.mult))
        nc.vector.scalar_tensor_tensor(out=out.bitcast(U32), in0=x.bitcast(U32), scalar=0x80000000, in1=low.bitcast(U32),
                                       op0=ALU.bitwise_and, op1=ALU.bitwise_or).then_inc(done, 1)


def fp4_network(c, base):
    nc = c.nc
    with ExitStack() as ctx:
        def sem(n): return c.sem("fp4_" + n)
        def sb(n, shape, dt=F32): return ctx.enter_context(nc.sbuf_tensor("fp4_" + n, shape, dt))
        W = load_stage(c, ctx, "s4")
        Q = Quantiser(c, ctx, "fp4_q_", TILES * HB)
        wq = sb("wq", [P, 9 * P])
        wt = sb("wt", [P, 9 * P])
        x_rows, xq_rows = sb("x_rows", [P, GROUP]), sb("xq_rows", [P, GROUP])
        xq = sb("xq", [P, GROUP])
        silu = sb("silu", [P, 2, FF4P])
        h = sb("h", [P, TILES, FF4P])
        hq_rows = sb("hq_rows", [P, TILES, FF4P])
        hq = sb("hq", [P, 3, GROUP])
        s_wq, s_wtp, s_wt = sem("weights_rounded"), sem("weights_turned"), sem("weights_moved")
        s_xr, s_xm, s_xq, s_xt, s_xtm = sem("x_rows"), sem("x_rows_moved"), sem("x_rounded"), sem("x_turned"), sem("x_moved")
        s_gu, s_silu, s_h = sem("gate_up_ready"), sem("silu_ready"), sem("h_ready")
        s_hq, s_ht, s_htm, s_rows = sem("h_rounded"), sem("h_turned"), sem("h_moved"), sem("rows_ready")
        bank = c.bank
        block = ctx.enter_context(nc.Block())

        @block.sync
        def _(sp):
            W.start(sp)

        @block.gpsimd
        def _(pool):
            with pool.Fori(0, GROUPS) as i:
                fetch_group(c, pool, i + base, i)
                norm_pool(c, pool, i + base)

        @block.tensor
        def _(pe):
            pe.wait_ge(s_wq, 1)
            for m in range(3):
                if m:
                    pe.wait_ge(s_wt, m)
                for k in range(3):
                    at = (3 * m + k) * P
                    last = nc.tensor.transpose(bank[1][:, k * P:(k + 1) * P], wq[:, at:at + P], c.ident)
                last.then_inc(s_wtp, 1)
            pe.wait_ge(s_wt, 3)
            with pe.Fori(0, GROUPS) as i:
                pe.wait_ge(c.s_cur, i + (base + 1))
                for t in range(TILES):
                    last = nc.tensor.transpose(bank[1][:, t * P:(t + 1) * P], c.cur[:, t * P:(t + 1) * P], c.ident)
                last.then_inc(s_xr, 1)
                pe.wait_ge(s_xq, i + 1)
                for t in range(TILES):
                    last = nc.tensor.transpose(bank[1][:, t * P:(t + 1) * P], xq_rows[:, t * P:(t + 1) * P], c.ident)
                last.then_inc(s_xt, 1)
                pe.wait_ge(s_xtm, i + 1)
                for t in range(TILES):
                    if t >= 2:
                        pe.wait_ge(s_h, i * TILES + (t - 1))
                    sl = slice(t * P, (t + 1) * P)
                    nc.tensor.matmul(bank[2 + t % 2][:, 0:FF4P], xq[:, sl], wt[:, 0:FF4P], start=True, stop=True)
                    nc.tensor.matmul(bank[4 + t % 2][:, 0:FF4P], xq[:, sl], wt[:, FF4P:2 * FF4P], start=True, stop=True).then_inc(s_gu, 1)
                pe.wait_ge(s_hq, i + 1)
                for k in range(3):
                    if k:
                        pe.wait_ge(s_htm, i * 3 + k)
                    for t in range(TILES):
                        last = nc.tensor.transpose(bank[1][:, t * P:(t + 1) * P], hq_rows[:, t, k * P:(k + 1) * P], c.ident)
                    last.then_inc(s_ht, 1)
                pe.wait_ge(s_htm, i * 3 + 3)
                for t in range(TILES):
                    sl = slice(t * P, (t + 1) * P)
                    nc.tensor.matmul(bank[6][:, sl], c.cur[:, sl], c.ident, start=True, stop=False)
                    for k in range(3):
                        last = nc.tensor.matmul(bank[6][:, sl], hq[:, k, sl], wt[:, (6 + k) * P:(7 + k) * P], start=False, stop=(k == 2))
                last.then_inc(s_rows, 1)
                norm_tensor(c, pe, i + base)

        @block.vector
        def _(dve):
            W.wait(dve)
            blocks = lambda a: a.rearrange("p (b k) -> p b k", k=BLK)
            Q.run(dve, 0, blocks(W["w"]), blocks(wq[:]), s_wq)
            rows = bank[6].rearrange("p (t d) -> p t d", t=TILES)
            with dve.Fori(0, GROUPS) as i:
                dve.wait_ge(s_xr, i + 1)
                nc.vector.tensor_copy(x_rows[:], bank[1]).then_inc(s_xm, 1)
                dve.wait_ge(s_xm, i + 1)
                Q.run(dve, i * 2 + 1, blocks(x_rows[:]), blocks(xq_rows[:]), s_xq)
                for t in range(TILES):
                    dve.wait_ge(s_silu, i * TILES + (t + 1))
                    nc.vector.tensor_tensor(h[:, t], silu[:, t % 2], bank[4 + t % 2][:, 0:FF4P], ALU.mult).then_inc(s_h, 1)
                dve.wait_ge(s_h, i * TILES + TILES)
                Q.run(dve, i * 2 + 2, blocks(h[:].rearrange("p t f -> p (t f)")), blocks(hq_rows[:].rearrange("p t f -> p (t f)")), s_hq)
                norm_vector(c, dve, i + base, rows, (s_rows, i + 1))

        @block.scalar
        def _(act):
            for m in range(3):
                act.wait_ge(s_wtp, m + 1)
                nc.scalar.activation(wt[:, m * FF4P:(m + 1) * FF4P], bank[1][:, 0:FF4P], ACT.Copy).then_inc(s_wt, 1)
            with act.Fori(0, GROUPS) as i:
                act.wait_ge(s_xt, i + 1)
                nc.scalar.activation(xq[:], bank[1], ACT.Copy).then_inc(s_xtm, 1)
                for t in range(TILES):
                    act.wait_ge(s_gu, i * TILES + (t + 1))
                    if t >= 2:
                        act.wait_ge(s_h, i * TILES + (t - 1))
                    nc.scalar.activation(silu[:, t % 2], bank[2 + t % 2][:, 0:FF4P], ACT.Silu).then_inc(s_silu, 1)
                for k in range(3):
                    act.wait_ge(s_ht, i * 3 + (k + 1))
                    nc.scalar.activation(hq[:, k], bank[1], ACT.Copy).then_inc(s_htm, 1)
                norm_scalar(c, act, i + base, ds(i * GROUP, GROUP))
    return base + GROUPS



KVH = 4
LAT = 64


def linear_attention(c, base):
    nc = c.nc
    with ExitStack() as ctx:
        def sem(n): return c.sem("lin_" + n)
        def sb(n, shape, dt=F32): return ctx.enter_context(nc.sbuf_tensor("lin_" + n, shape, dt))
        W = load_stage(c, ctx, "s5")
        q, k = sb("q", [P, HT, GROUP]), sb("k", [P, HT, 4, GROUP])
        key = sb("key", [P, GROUP])
        v = sb("v", [P, TILES, KVH, 32])
        o_t = sb("o_t", [P, HT, S])
        below, above = sb("below", [P, 2, GROUP]), sb("above", [P, 2, GROUP])
        lat1, lat2 = sb("lat1", [32, 2, GROUP]), sb("lat2", [LAT, 2, GROUP])
        e = sb("e", [P, 2, JT, HT, S])
        num, rec = sb("num", [P, JT * HEADS, VW]), sb("rec", [P, JT * HEADS])
        att, att_t = sb("att", [P, TILES, D]), sb("att_t", [P, GROUP])
        inner = sb("inner", [P, GROUP])
        both = sb("both", [P, GROUP])
        s_ones = sem("ones_filled")
        s_proj, s_below, s_above, s_exp, s_feat = sem("proj_ready"), sem("below_ready"), sem("above_ready"), sem("exp_ready"), sem("features_ready")
        s_lat, s_latm = sem("latent_ready"), sem("latent_moved")
        s_vp, s_v, s_sc, s_e, s_pv = sem("vproj_ready"), sem("v_moved"), sem("scores_ready"), sem("scores_masked"), sem("pv_ready")
        s_num, s_den, s_rec, s_att, s_att_t, s_att_tm = sem("num_ready"), sem("den_ready"), sem("rec_ready"), sem("att_ready"), sem("att_turned"), sem("att_moved")
        s_key, s_zero, s_ot, s_o = sem("key_ready"), sem("v_zeroed"), sem("sums_moved"), sem("sums_turned")
        s_rows, s_rows2 = sem("rows_ready"), sem("sum_rows_ready")
        bank = c.bank
        both_banks = c.psum[:, 3072:4096]
        o = both_banks.rearrange("p (t q) -> p t q", t=HT)
        score = [c.psum[:, 1024:2048].rearrange("p (t q) -> p t q", t=HT), bank[4].rearrange("p (t q) -> p t q", t=HT)]
        U = 2 * HT
        block = ctx.enter_context(nc.Block())

        @block.sync
        def _(sp):
            W.start(sp)

        @block.gpsimd
        def _(pool):
            nc.gpsimd.memset(v[:], 0.0).then_inc(s_zero, 1)
            pool.wait_ge(s_zero, 1)
            nc.gpsimd.memset(v[:].rearrange("p t h v -> p (t h) v")[:, :, 0:1], 1.0).then_inc(s_ones, 1)
            with pool.Fori(0, GROUPS) as i:
                n = i * 2 + base
                fetch_group(c, pool, n, i)
                norm_pool(c, pool, n)
                norm_pool(c, pool, n + 1)

        @block.tensor
        def _(pe):
            W.wait(pe)
            pe.wait_ge(s_ones, 1)
            with pe.Fori(0, GROUPS) as i:
                n = i * 2 + base
                pe.wait_ge(c.s_cur, n + 1)
                for w in range(2):
                    nc.tensor.matmul(bank[6 + w][0:32], W["wkv"][:, 32 * w:32 * w + 32], c.cur[:], start=True, stop=True).then_inc(s_lat, 1)
                for w in range(2):
                    pe.wait_ge(s_latm, i * 4 + (w + 1))
                    nc.tensor.matmul(bank[6 + w][0:LAT], W["wc"][0:32], lat1[:, w], start=True, stop=True).then_inc(s_lat, 1)
                pe.wait_ge(s_latm, i * 4 + 4)
                for t in range(TILES):
                    last = nc.tensor.matmul(bank[6][:, t * 32:(t + 1) * 32], lat2[:, 1, t * P:(t + 1) * P], W["we"][0:LAT], start=True, stop=True)
                last.then_inc(s_vp, 1)
                for m in range(U):
                    b = bank[4 + m % 2]
                    if m >= 2:
                        pe.wait_ge(s_above, i * U + (m - 1))
                        pe.wait_ge(s_below, i * U + (m - 1))
                    T = m % HT
                    if m < HT:
                        nc.tensor.matmul(b, W["wepad"][0:LAT, T * P:(T + 1) * P], lat2[:, 0], start=True, stop=True).then_inc(s_proj, 1)
                    else:
                        nc.tensor.matmul(b, W["wq"][:, T * P:(T + 1) * P], c.cur[:], start=True, stop=True).then_inc(s_proj, 1)
                pe.wait_ge(s_feat, i * U + U)
                pe.wait_ge(s_v, i + 1)

                def scores(s, g):
                    for ch in range(JT):
                        u = (s * 4 + g) * 2 + ch
                        a = ch * P
                        if u >= 2:
                            pe.wait_ge(s_e, i * 16 + (u - 1))
                        for T in range(HT):
                            last = nc.tensor.matmul(score[ch][:, T], k[:, T, g, s * S + a:s * S + a + P], q[:, T, s * S + a:(s + 1) * S], start=True, stop=True)
                        last.then_inc(s_sc, 1)

                def values(s, g):
                    pe.wait_ge(s_e, i * 16 + ((s * 4 + g) * 2 + 2))
                    for T in range(HT):
                        for ch in range(JT):
                            last = nc.tensor.matmul(o[32 * g:32 * g + 32, T, ch * P:S], v[:, s * JT + ch, T], e[:, g % 2, ch, T, ch * P:S],
                                                    start=(ch == 0), stop=True, skip_group_check=(ch > 0))
                    last.then_inc(s_pv, 1)

                for s in range(SEQ_G):
                    for g in range(4):
                        if g or not s:
                            scores(s, g)
                        if g >= 1:
                            values(s, g - 1)
                    values(s, 3)
                    pe.wait_ge(s_ot, i * SEQ_G + (s + 1))
                    for j in range(JT):
                        for T in range(HT):
                            at = (j * HT + T) * P
                            last = nc.tensor.transpose(both_banks[:, at:at + P], o_t[:, T, j * P:(j + 1) * P], c.ident)
                    last.then_inc(s_o, 1)
                    if s + 1 < SEQ_G:
                        scores(s + 1, 0)
                    pe.wait_ge(s_num, i * SEQ_G + (s + 1))
                pe.wait_ge(s_att, i * SEQ_G + SEQ_G)
                for t in range(TILES):
                    last = nc.tensor.transpose(bank[5][:, t * P:(t + 1) * P], att[:, t, :], c.ident)
                last.then_inc(s_att_t, 1)
                pe.wait_ge(s_att_tm, i + 1)
                for t in range(TILES):
                    sl = slice(t * P, (t + 1) * P)
                    nc.tensor.matmul(bank[6][:, sl], att_t[:, sl], W["wo"], start=True, stop=False)
                    nc.tensor.matmul(bank[6][:, sl], c.ones[0:1, 0:P], W["bo"][0:1], start=False, stop=False)
                    last = nc.tensor.matmul(bank[6][:, sl], c.cur[:, sl], c.ident, start=False, stop=True)
                last.then_inc(s_rows, 1)
                norm_tensor(c, pe, n)
                pe.wait_ge(c.s_cur, n + 2)
                for t in range(TILES):
                    last = nc.tensor.transpose(bank[6][:, t * P:(t + 1) * P], both[:, t * P:(t + 1) * P], c.ident)
                last.then_inc(s_rows2, 1)
                norm_tensor(c, pe, n + 1)

        @block.vector
        def _(dve):
            W.wait(dve)
            rows = bank[6].rearrange("p (t d) -> p t d", t=TILES)
            with dve.Fori(0, GROUPS) as i:
                n = i * 2 + base
                for w in range(2):
                    dve.wait_ge(s_lat, i * 4 + (w + 1))
                    nc.vector.tensor_scalar(lat1[:, w], bank[6 + w][0:32], W["bkv"][0:32, w:w + 1], None, ALU.add).then_inc(s_latm, 1)
                for w in range(2):
                    dve.wait_ge(s_lat, i * 4 + (w + 3))
                    nc.vector.tensor_copy(lat2[:, w], bank[6 + w][0:LAT]).then_inc(s_latm, 1)
                dve.wait_ge(s_vp, i + 1)
                nc.vector.tensor_copy(v[:].rearrange("p t h v -> p (t h) v")[:, :, 1:VW],
                                      bank[6][:, 0:P].rearrange("p (h d) -> p h d", d=HD)).then_inc(s_v, 1)

                def finish_map(m):
                    dve.wait_ge(s_exp, i * U + (m + 1))
                    T = m % HT
                    if m < HT:
                        nc.vector.tensor_tensor(key[:], above[:, m % 2], below[:, m % 2], ALU.add).then_inc(s_key, 1)
                        dve.wait_ge(s_key, i * HT + (T + 1))
                        for g in range(4):
                            last = nc.vector.tensor_scalar(k[:, T, g], key[:], W["heads"][:, g:g + 1], None, ALU.mult)
                        last.then_inc(s_feat, 1)
                    else:
                        nc.vector.tensor_tensor(q[:, T], above[:, m % 2], below[:, m % 2], ALU.add).then_inc(s_feat, 1)

                for m in range(U):
                    dve.wait_ge(s_proj, i * U + (m + 1))
                    if m >= 2:
                        finish_map(m - 2)
                        dve.wait_ge(s_feat, i * U + (m - 1))
                    b = bank[4 + m % 2]
                    bias = W["bq"][:, m % HT:m % HT + 1] if m >= HT else 0.0
                    nc.vector.tensor_scalar(below[:, m % 2], b, bias, 0.0, ALU.add, ALU.min).then_inc(s_below, 1)
                    nc.vector.tensor_scalar(above[:, m % 2], b, bias, 0.0, ALU.add, ALU.max).then_inc(s_above, 1)
                finish_map(U - 2)
                finish_map(U - 1)
                mask = W["tri"].rearrange("p (c q) -> p c q", c=JT)
                for s in range(SEQ_G):
                    for g in range(4):
                        if s * 4 + g >= 2:
                            dve.wait_ge(s_pv, i * 8 + (s * 4 + g - 1))
                        for ch in range(JT):
                            u = (s * 4 + g) * 2 + ch
                            a = ch * P
                            dve.wait_ge(s_sc, i * 16 + (u + 1))
                            nc.vector.tensor_tensor(e[:, g % 2, ch, :, a:S], score[ch], mask[:, ch:ch + 1, a:S].broadcast_to([P, HT, S - a]), ALU.mult)\
                                .then_inc(s_e, 1)
                    dve.wait_ge(s_o, i * SEQ_G + (s + 1))
                    nc.vector.tensor_copy(num[:], both_banks.rearrange("p (h v) -> p h v", v=32)[:, :, 0:VW]).then_inc(s_num, 1)
                    dve.wait_ge(s_num, i * SEQ_G + (s + 1))
                    nc.vector.tensor_scalar(rec[:].unsqueeze(2), num[:, :, 0:1], 1e-6, None, ALU.add).then_inc(s_den, 1)
                    dve.wait_ge(s_den, i * SEQ_G + (s + 1))
                    nc.vector.reciprocal(rec[:], rec[:]).then_inc(s_rec, 1)
                    dve.wait_ge(s_rec, i * SEQ_G + (s + 1))
                    out = att[:, s * JT:(s + 1) * JT, :].rearrange("p j (h d) -> p (j h) d", h=HEADS)
                    nc.vector.tensor_tensor(out, num[:, :, 1:VW], rec[:].unsqueeze(2).broadcast_to([P, JT * HEADS, HD]), ALU.mult).then_inc(s_att, 1)
                norm_vector(c, dve, n, rows, (s_rows, i + 1))
                dve.wait_ge(c.s_done, n + 2)
                nc.vector.tensor_tensor(both[:], inner[:], c.cur[:], ALU.add).then_inc(c.s_cur, 1)
                norm_vector(c, dve, n + 1, rows, (s_rows2, i + 1))

        @block.scalar
        def _(act):
            W.wait(act)
            with act.Fori(0, GROUPS) as i:
                n = i * 2 + base
                for m in range(U):
                    act.wait_ge(s_below, i * U + (m + 1))
                    act.wait_ge(s_above, i * U + (m + 1))
                    nc.scalar.activation(below[:, m % 2], below[:, m % 2], ACT.Exp, bias=W["off"][:, 0:1] if m < HT else 0.0).then_inc(s_exp, 1)
                for s in range(SEQ_G):
                    act.wait_ge(s_pv, i * 8 + (s * 4 + 4))
                    nc.scalar.activation(o_t[:].rearrange("p t q -> p (t q)"), both_banks, ACT.Copy).then_inc(s_ot, 1)
                act.wait_ge(s_att_t, i + 1)
                nc.scalar.activation(att_t[:], bank[5], ACT.Copy).then_inc(s_att_tm, 1)
                act.wait_ge(c.s_turned, n + 1)
                nc.scalar.activation(inner[:], c.turned, ACT.Identity, bias=W["beta"], scale=W["gamma"]).then_inc(c.s_done, 1)
                norm_scalar(c, act, n + 1, ds(i * GROUP, GROUP))
    return base + 2 * GROUPS



def ternary_network(c, base):
    nc = c.nc
    with ExitStack() as ctx:
        def sem(n): return c.sem("ter_" + n)
        def sb(n, shape, dt=F32): return ctx.enter_context(nc.sbuf_tensor("ter_" + n, shape, dt))
        W = load_stage(c, ctx, "s6")
        silu = sb("silu", [P, 2, GROUP])
        h0, h1, h2 = (sb(n, [P, FC, GROUP]) for n in ("h0", "h1", "h2"))
        y = sb("y", [P, GROUP])
        s_up, s_silu, s_h0 = sem("up_ready"), sem("silu_ready"), sem("h0_ready")
        s_p, s_g, s_y, s_sum, s_rows = sem("product_ready"), sem("gelu_ready"), sem("y_ready"), sem("sum_ready"), sem("rows_ready")
        bank = c.bank
        block = ctx.enter_context(nc.Block())

        @block.sync
        def _(sp):
            W.start(sp)

        @block.gpsimd
        def _(pool):
            with pool.Fori(0, GROUPS) as i:
                fetch_group(c, pool, i + base, i)
                norm_pool(c, pool, i + base)

        @block.tensor
        def _(pe):
            W.wait(pe)
            with pe.Fori(0, GROUPS) as i:
                pe.wait_ge(c.s_cur, i + (base + 1))
                for f in range(FC):
                    if f >= 2:
                        pe.wait_ge(s_h0, i * FC + (f - 1))
                    nc.tensor.matmul(bank[1 + f % 2], W["w1"][:, f * P:(f + 1) * P], c.cur[:], start=True, stop=True)
                    nc.tensor.matmul(bank[3 + f % 2], W["w2"][:, f * P:(f + 1) * P], c.cur[:], start=True, stop=True).then_inc(s_up, 1)
                for layer, (w, src) in enumerate((("h1", h0), ("h2", h1))):
                    wt = W[w].rearrange("p (k n) -> p k n", k=FC)
                    for f in range(FC):
                        m = layer * FC + f
                        if m >= 2:
                            pe.wait_ge(s_g, i * (2 * FC) + (m - 1))
                        for kk in range(FC):
                            if layer == 0 and f == 0:
                                pe.wait_ge(s_h0, i * FC + (kk + 1))
                            if layer == 1 and f == 0:
                                pe.wait_ge(s_g, i * (2 * FC) + (kk + 1))
                            last = nc.tensor.matmul(bank[5 + f % 2], wt[:, kk, f * P:(f + 1) * P], src[:, kk], start=(kk == 0), stop=(kk == FC - 1))
                        last.then_inc(s_p, 1)
                for kk in range(FC):
                    pe.wait_ge(s_g, i * (2 * FC) + (FC + kk + 1))
                    last = nc.tensor.matmul(bank[7], W["w3"][:, kk * P:(kk + 1) * P], h2[:, kk], start=(kk == 0), stop=(kk == FC - 1))
                last.then_inc(s_y, 1)
                pe.wait_ge(s_sum, i + 1)
                for t in range(TILES):
                    last = nc.tensor.transpose(bank[1][:, t * P:(t + 1) * P], y[:, t * P:(t + 1) * P], c.ident)
                last.then_inc(s_rows, 1)
                norm_tensor(c, pe, i + base)

        @block.vector
        def _(dve):
            W.wait(dve)
            rows = bank[1].rearrange("p (t d) -> p t d", t=TILES)
            with dve.Fori(0, GROUPS) as i:
                for f in range(FC):
                    dve.wait_ge(s_silu, i * FC + (f + 1))
                    nc.vector.scalar_tensor_tensor(out=h0[:, f], in0=bank[3 + f % 2], scalar=W["s2"][:, f:f + 1], in1=silu[:, f % 2],
                                                   op0=ALU.mult, op1=ALU.mult).then_inc(s_h0, 1)
                dve.wait_ge(s_y, i + 1)
                nc.vector.scalar_tensor_tensor(out=y[:], in0=bank[7], scalar=W["s3"], in1=c.cur[:], op0=ALU.mult, op1=ALU.add).then_inc(s_sum, 1)
                norm_vector(c, dve, i + base, rows, (s_rows, i + 1))

        @block.scalar
        def _(act):
            W.wait(act)
            with act.Fori(0, GROUPS) as i:
                for f in range(FC):
                    if f >= 2:
                        act.wait_ge(s_h0, i * FC + (f - 1))
                    act.wait_ge(s_up, i * FC + (f + 1))
                    nc.scalar.activation(silu[:, f % 2], bank[1 + f % 2], ACT.Silu, scale=W["s1"][:, f:f + 1]).then_inc(s_silu, 1)
                for m in range(2 * FC):
                    f = m % FC
                    act.wait_ge(s_p, i * (2 * FC) + (m + 1))
                    nc.scalar.activation((h1, h2)[m // FC][:, f], bank[5 + f % 2], ACT.Gelu, scale=W["hs"][:, m:m + 1]).then_inc(s_g, 1)
                norm_scalar(c, act, i + base, ds(i * GROUP, GROUP))
    return base + GROUPS


UNROLL = 8
HALF = UNROLL // 2


def delta_rule(c, base):
    nc = c.nc
    with ExitStack() as ctx:
        def sem(n): return c.sem("del_" + n)
        def sb(n, shape, dt=F32, ctx=ctx): return ctx.enter_context(nc.sbuf_tensor("del_" + n, shape, dt))
        W = load_stage(c, ctx, "s3")
        q_all, k_all, ka_all, dec_all = (sb(n, [P, SEQS, S]) for n in ("q_all", "k_all", "ka_all", "dec_all"))
        bv_all = sb("bv_all", [P, SEQS, S + UNROLL])
        pn_all = sb("pn_all", [P, TOKENS])
        bank = c.bank
        g0 = lambda i: ds(i * SEQ_G, SEQ_G)
        delta_inputs(c, base, W, q_all, k_all, ka_all, dec_all, bv_all, pn_all)
        o_all = sb("o_all", [P, SEQS, S])
        delta_scan(c, W, q_all, k_all, ka_all, dec_all, bv_all, o_all)
        delta_output(c, base, W, pn_all, o_all)
    return base + GROUPS


def delta_inputs(c, base, W, q_all, k_all, ka_all, dec_all, bv_all, pn_all):
    nc = c.nc
    with ExitStack() as ctx:
        def sem(n): return c.sem("din_" + n)
        def sb(n, shape, dt=F32): return ctx.enter_context(nc.sbuf_tensor("din_" + n, shape, dt))
        cos, sin, rad = sb("cos", [P, S]), sb("sin", [P, S]), sb("rad", [P, S])
        w = sb("w", [P, 16])
        turns, half_sin, half_cos = sb("turns", [P, S]), sb("half_sin", [P, S]), sb("half_cos", [P, S])
        tmp = sb("tmp", [P, GROUP])
        zin, z, y, sq = sb("zin", [P, GROUP]), sb("z", [P, GROUP]), sb("y", [P, GROUP]), sb("sq", [P, GROUP])
        t2 = sb("t2", [P, GROUP])
        root, pn = sb("root", [P, GROUP]), sb("pn", [P, GROUP])
        padded = sb("padded", [P, 3, SEQ_G, S + 3])
        conv = sb("conv", [P, 3, GROUP])
        gates = sb("gates", [P, 2, GROUP])
        inv = sb("inv", [P, GROUP])
        ramp = sb("ramp", [P, 1])
        s_tab, s_trig, s_dec = sem("table_step"), sem("trig_step"), sem("decay_step")
        s_pe, s_dve, s_act = sem("product_ready"), sem("vector_step"), sem("activation_ready")
        s_cur = sem("group_fetched")
        s_moved = sem("normed_kept")
        s_out = sem("group_through")
        s_fill = sem("filled")
        bank = c.bank
        PE_N, DVE_N, ACT_N = 13, 33, 14
        block = ctx.enter_context(nc.Block())
        seqs = lambda a: a.rearrange("p (b t) -> p b t", b=SEQ_G)
        both = lambda a: a[:].unsqueeze(1).broadcast_to([P, SEQ_G, S])

        @block.sync
        def _(sp):
            W.start(sp)

        @block.gpsimd
        def _(pool):
            nc.gpsimd.memset(padded[:], 0.0)
            nc.gpsimd.memset(bv_all[:], 0.0).then_inc(s_fill, 1)
            pool.wait_ge(c.s_done, base + 1)
            with pool.Fori(0, GROUPS) as i:
                pool.wait_ge(s_out, i + 1)
                nc.gpsimd.tensor_copy(c.cur[:], c.H[:, ds(i * GROUP, GROUP)]).then_inc(s_cur, 1)
                pool.wait_ge(s_dve, i * DVE_N + 9)
                nc.gpsimd.tensor_copy(pn_all[:, ds(i * GROUP, GROUP)], pn[:]).then_inc(s_moved, 1)

        @block.tensor
        def _(pe):
            W.wait(pe)
            with pe.Fori(0, GROUPS) as i:
                def mm(k, b, lhs, rhs):
                    nc.tensor.matmul(bank[b], lhs, rhs, start=True, stop=True).then_inc(s_pe, 1)
                pe.wait_ge(s_cur, i + 1)
                mm(1, 1, W["partner"], c.cur[:])
                for j in range(3):
                    mm(2 + j, 2 + j, W["ctrl"][:, j * P:(j + 1) * P], c.cur[:])
                mm(5, 5, W["dec"], c.cur[:])
                mm(6, 6, W["beta"], c.cur[:])
                pe.wait_ge(s_dve, i * DVE_N + 4)
                mm(7, 1, W["partner"], z[:])
                pe.wait_ge(s_act, i * ACT_N + 6)
                mm(8, 7, c.ones[:], sq[:])
                pe.wait_ge(s_act, i * ACT_N + 7)
                pe.wait_ge(s_dve, i * DVE_N + 9)
                for j in range(3):
                    mm(9 + j, 2 + j, W["p20c"][:, j * P:(j + 1) * P], pn[:])
                for j in range(2):
                    pe.wait_ge(s_act, i * ACT_N + (11 + 2 * j))
                    mm(12 + j, 7, W["bones"], sq[:])

        @block.vector
        def _(dve):
            W.wait(dve)
            V = nc.vector

            def tab(k, ins):
                ins.then_inc(s_tab, 1)
                dve.wait_ge(s_tab, k)

            MAGIC = 1.5 * 2.0 ** 23
            high, low = w[:, 0:1], w[:, 1:2]
            tab(1, V.tensor_scalar(high.bitcast(U32), W["theta"].bitcast(U32), 0xFFFFF000, None, ALU.bitwise_and))
            V.tensor_tensor(low, W["theta"], high, ALU.subtract)
            tab(2, V.tensor_scalar(cos[:], W["time"], high, None, ALU.mult))
            tab(3, V.tensor_scalar(turns[:], cos[:], 1.0 / (2 * np.pi), MAGIC, ALU.mult, ALU.add))
            tab(4, V.tensor_scalar(turns[:], turns[:], MAGIC, None, ALU.subtract))
            for k in range(3):
                tab(5 + k, V.scalar_tensor_tensor(out=cos[:], in0=turns[:], scalar=-TWO_PI[k], in1=cos[:], op0=ALU.mult, op1=ALU.add))
            tab(8, V.scalar_tensor_tensor(out=cos[:], in0=W["time"], scalar=low, in1=cos[:], op0=ALU.mult, op1=ALU.add))
            tab(9, V.tensor_scalar(sin[:], cos[:], 0.5, None, ALU.mult))
            tab(10, V.tensor_scalar(turns[:].bitcast(U32), sin[:].bitcast(U32), 0x7FFFFFFF, None, ALU.bitwise_and))
            tab(11, V.tensor_scalar(turns[:], turns[:], -1.0, float(np.float32(np.pi / 2)), ALU.mult, ALU.add))
            dve.wait_ge(s_trig, 2)
            V.tensor_tensor(cos[:], half_sin[:], half_sin[:], ALU.mult)
            tab(12, V.tensor_tensor(sin[:], half_sin[:], half_cos[:], ALU.mult))
            V.tensor_scalar(cos[:], cos[:], -2.0, 1.0, ALU.mult, ALU.add)
            tab(13, V.tensor_scalar(sin[:], sin[:], 2.0, None, ALU.mult))
            n = 13
            dve.wait_ge(s_dec, 2)
            V.memset(tmp[:, 0:S], 0.0).then_inc(s_tab, 1)
            dve.wait_ge(s_tab, n + 1)
            V.tensor_scalar(rad[:], tmp[:, 0:S], w[:, 11:12], None, ALU.add).then_inc(s_out, 1)
            dve.wait_ge(s_fill, 1)
            dve.wait_ge(s_out, 1)
            dve.wait_ge(s_trig, 3)

            with dve.Fori(0, GROUPS) as i:
                def step(k, ins, wait=True):
                    ins.then_inc(s_dve, 1)
                    if wait:
                        dve.wait_ge(s_dve, i * DVE_N + k)
                dve.wait_ge(s_pe, i * PE_N + 1)
                step(1, V.tensor_tensor(seqs(tmp[:]), seqs(bank[1]), both(sin), ALU.mult), wait=False)
                step(2, V.tensor_tensor(seqs(zin[:]), seqs(c.cur[:]), both(cos), ALU.mult))
                step(3, V.tensor_tensor(zin[:], zin[:], tmp[:], ALU.add))
                V.tensor_tensor_scan(z[:, 0:S], rad[:], zin[:, 0:S], 0.0, ALU.mult, ALU.add)
                step(4, V.tensor_tensor_scan(z[:, S:GROUP], rad[:], zin[:, S:GROUP], 0.0, ALU.mult, ALU.add))
                dve.wait_ge(s_pe, i * PE_N + 7)
                step(5, V.tensor_tensor(seqs(tmp[:]), seqs(bank[1]), both(sin), ALU.mult), wait=False)
                step(6, V.tensor_tensor(seqs(zin[:]), seqs(z[:]), both(cos), ALU.mult))
                step(7, V.tensor_tensor(y[:], zin[:], tmp[:], ALU.subtract))
                dve.wait_ge(s_act, i * ACT_N + 7)
                step(8, V.reciprocal(inv[:], root[:]))
                step(9, V.scalar_tensor_tensor(out=pn[:], in0=y[:], scalar=W["vnorm"], in1=inv[:], op0=ALU.mult, op1=ALU.mult))
                n = 9
                for j in range(3):
                    for tap in range(4):
                        x = padded[:, j, :, tap:tap + S]
                        wt = W["conv"][:, 4 * j + tap:4 * j + tap + 1]
                        n += 1
                        if tap == 0:
                            step(n, V.tensor_scalar(seqs(conv[:, j]), x, wt, None, ALU.mult))
                        else:
                            step(n, V.scalar_tensor_tensor(out=seqs(conv[:, j]), in0=x, scalar=wt, in1=seqs(conv[:, j]), op0=ALU.mult, op1=ALU.add))
                for j in range(3):
                    dve.wait_ge(s_pe, i * PE_N + (9 + j))
                    dve.wait_ge(s_act, i * ACT_N + (8 + j))
                    n += 1
                    step(n, V.scalar_tensor_tensor(out=conv[:, j], in0=bank[2 + j], scalar=ramp[:], in1=conv[:, j], op0=ALU.mult, op1=ALU.add))
                n += 1
                dve.wait_ge(s_act, i * ACT_N + 5)
                step(n, V.tensor_copy(dec_all[:, ds(i * SEQ_G, SEQ_G), :], seqs(gates[:, 0])))
                n += 1
                step(n, V.tensor_tensor(bv_all[:, ds(i * SEQ_G, SEQ_G), 0:S], seqs(conv[:, 2]), seqs(gates[:, 1]), ALU.mult))
                n += 1
                step(n, V.tensor_tensor(gates[:, 1], gates[:, 0], gates[:, 1], ALU.mult))
                for j in range(2):
                    dve.wait_ge(s_act, i * ACT_N + (12 + 2 * j))
                    n += 1
                    step(n, V.reciprocal(inv[:], root[:]))
                    n += 1
                    if j == 0:
                        step(n, V.scalar_tensor_tensor(out=q_all[:, ds(i * SEQ_G, SEQ_G), :], in0=seqs(conv[:, 0]), scalar=HD ** -0.5,
                                                       in1=seqs(inv[:]), op0=ALU.mult, op1=ALU.mult))
                    else:
                        step(n, V.tensor_tensor(zin[:], conv[:, 1], inv[:], ALU.mult))
                n += 1
                step(n, V.tensor_copy(k_all[:, ds(i * SEQ_G, SEQ_G), :], seqs(zin[:])))
                n += 1
                step(n, V.tensor_tensor(ka_all[:, ds(i * SEQ_G, SEQ_G), :], seqs(zin[:]), seqs(gates[:, 1]), ALU.mult))
                assert n == DVE_N, n
                dve.wait_ge(s_moved, i + 1)
                V.memset(tmp[:, 0:1], 0.0).then_inc(s_out, 1)

        @block.scalar
        def _(act):
            W.wait(act)
            SC = nc.scalar
            act.wait_ge(s_tab, 11)
            SC.activation(half_sin[:], sin[:], ACT.Sin).then_inc(s_trig, 1)
            SC.activation(half_cos[:], turns[:], ACT.Sin).then_inc(s_trig, 1)
            SC.activation(w[:, 12:13], W["decay"], ACT.Exp).then_inc(s_dec, 1)
            act.wait_ge(s_dec, 1)
            SC.activation(w[:, 11:12], w[:, 12:13], ACT.Exp, scale=-1.0).then_inc(s_dec, 1)
            SC.activation(ramp[:], W["ramp"], ACT.Sigmoid).then_inc(s_trig, 1)
            act.wait_ge(s_fill, 1)
            with act.Fori(0, GROUPS) as i:
                def do(k, *a, **kw):
                    SC.activation(*a, **kw).then_inc(s_act, 1)
                for j in range(3):
                    act.wait_ge(s_pe, i * PE_N + (2 + j))
                    do(1 + j, padded[:, j, :, 3:S + 3], seqs(bank[2 + j]), ACT.Identity, bias=W["bctrl"][:, j:j + 1])
                act.wait_ge(s_pe, i * PE_N + 5)
                do(4, gates[:, 0], bank[5], ACT.Sigmoid, bias=W["bctrl"][:, 3:4])
                act.wait_ge(s_pe, i * PE_N + 6)
                do(5, gates[:, 1], bank[6], ACT.Sigmoid, bias=W["bctrl"][:, 4:5])
                act.wait_ge(s_dve, i * DVE_N + 7)
                do(6, sq[:], y[:], ACT.Square)
                act.wait_ge(s_pe, i * PE_N + 8)
                do(7, root[:], bank[7], ACT.Sqrt, scale=1.0 / D, bias=W["eps"])
                for j in range(3):
                    act.wait_ge(s_dve, i * DVE_N + (9 + 4 * (j + 1)))
                    do(8 + j, conv[:, j], conv[:, j], ACT.Silu)
                for j in range(2):
                    act.wait_ge(s_dve, i * DVE_N + (22 + j))
                    if j == 1:
                        act.wait_ge(s_pe, i * PE_N + 12)
                    do(11 + 2 * j, sq[:], conv[:, j], ACT.Square)
                    act.wait_ge(s_pe, i * PE_N + (12 + j))
                    if j == 1:
                        act.wait_ge(s_dve, i * DVE_N + 28)
                    do(12 + 2 * j, root[:], bank[7], ACT.Sqrt, bias=W["eps"])


def delta_scan(c, W, q_all, k_all, ka_all, dec_all, bv_all, o_all):
    nc = c.nc
    with ExitStack() as ctx:
        def sem(n): return c.sem("rule_" + n)
        def sb(n, shape, dt=F32): return ctx.enter_context(nc.sbuf_tensor("rule_" + n, shape, dt))
        states = sb("states", [P, UNROLL, SEQS, HD])
        against = sb("against", [P, SEQS, HD])
        asked = sb("asked", [P, UNROLL, SEQS, HD])
        outer = sb("outer", [P, SEQS, HD])
        decayed = sb("decayed", [P, SEQS, HD])
        marks = sb("marks", [P, 2])
        s_state, s_against, s_err, s_outer, s_decayed = sem("state_ready"), sem("against_ready"), sem("error_ready"), sem("outer_ready"), sem("decayed")
        s_asked, s_read, s_kept = sem("asked_ready"), sem("read_ready"), sem("read_kept")
        bank = c.bank
        errs = [bank[b].rearrange("p (t b v) -> p t b v", t=HALF, b=SEQS) for b in (1, 2)]
        read = bank[3][:, 0:UNROLL * SEQS].rearrange("p (t b) -> p t b", t=UNROLL)
        vec = lambda a, i, k: a[:, :, ds(i * UNROLL + k, 1)].broadcast_to([P, SEQS, HD])
        block = ctx.enter_context(nc.Block())

        @block.gpsimd
        def _(pool):
            nc.gpsimd.memset(states[:, UNROLL - 1], 0.0).then_inc(s_state, 1)
            nc.gpsimd.memset(marks[:, 0:1], 0.0).then_inc(s_read, 1)
            nc.gpsimd.memset(marks[:, 1:2], 0.0).then_inc(s_kept, 1)
            with pool.Fori(0, S // UNROLL) as i:
                for k in range(UNROLL):
                    pool.wait_ge(s_state, i * UNROLL + (k + 1))
                    nc.gpsimd.tensor_tensor(decayed[:], states[:, (k - 1) % UNROLL], vec(dec_all, i, k), ALU.mult).then_inc(s_decayed, 1)

        @block.tensor
        def _(pe):
            def want(i, half, at):
                cols = bv_all[:, :, ds(i * UNROLL + at, HALF)].rearrange("p b t -> p t b")
                for v in range(HD):
                    nc.tensor.matmul(errs[half][:, :, :, v], W["spread"][:, v * P:(v + 1) * P], cols, start=(v == 0), stop=True,
                                     skip_group_check=(v > 0))
            want(0, 0, 0)
            with pe.Fori(0, S // UNROLL) as i:
                for k in range(UNROLL):
                    pe.wait_ge(s_against, i * UNROLL + (k + 1))
                    nc.tensor.matmul(errs[k // HALF][:, k % HALF].rearrange("p b v -> p (b v)"), W["minus_bones"],
                                     against[:].rearrange("p b v -> p (b v)"), start=False, stop=True, skip_group_check=True).then_inc(s_err, 1)
                    if k == 0:
                        want(i, 1, HALF)
                    if k == HALF:
                        want(i, 0, UNROLL)
                pe.wait_ge(s_asked, i * UNROLL + UNROLL)
                pe.wait_ge(s_kept, i + 1)
                for v in range(HD):
                    last = nc.tensor.matmul(read, W["gather"][:, v * P:(v + 1) * P], asked[:, :, :, v], start=(v == 0), stop=(v == HD - 1))
                last.then_inc(s_read, 1)

        @block.vector
        def _(dve):
            V = nc.vector
            with dve.Fori(0, S // UNROLL) as i:
                def ask(k):
                    if k == 0:
                        dve.wait_ge(s_read, i + 1)
                    V.tensor_tensor(asked[:, k], states[:, k], vec(q_all, i, k), ALU.mult).then_inc(s_asked, 1)

                for k in range(UNROLL):
                    dve.wait_ge(s_state, i * UNROLL + (k + 1))
                    V.tensor_tensor(against[:], states[:, (k - 1) % UNROLL], vec(ka_all, i, k), ALU.mult).then_inc(s_against, 1)
                    if k:
                        ask(k - 1)
                    dve.wait_ge(s_err, i * UNROLL + (k + 1))
                    V.tensor_tensor(outer[:], errs[k // HALF][:, k % HALF], vec(k_all, i, k), ALU.mult).then_inc(s_outer, 1)
                    dve.wait_ge(s_outer, i * UNROLL + (k + 1))
                    dve.wait_ge(s_decayed, i * UNROLL + (k + 1))
                    V.tensor_tensor(states[:, k], decayed[:], outer[:], ALU.add).then_inc(s_state, 1)
                dve.wait_ge(s_state, i * UNROLL + (UNROLL + 1))
                ask(UNROLL - 1)

        @block.scalar
        def _(act):
            with act.Fori(0, S // UNROLL) as i:
                act.wait_ge(s_read, i + 2)
                nc.scalar.activation(o_all[:, :, ds(i * UNROLL, UNROLL)].rearrange("p b t -> p t b"), read, ACT.Copy).then_inc(s_kept, 1)


def delta_output(c, base, W, pn_all, o_all):
    nc = c.nc
    with ExitStack() as ctx:
        def sem(n): return c.sem("dout_" + n)
        def sb(n, shape, dt=F32): return ctx.enter_context(nc.sbuf_tensor("dout_" + n, shape, dt))
        o, pn, sq, root, inv, nr = (sb(n, [P, GROUP]) for n in ("o", "pn", "sq", "root", "inv", "nr"))
        gate, y = sb("gate", [P, TILES, D]), sb("y", [P, TILES, D])
        s_o, s_sq, s_sum, s_root, s_inv, s_nr = sem("o_fetched"), sem("squared"), sem("summed"), sem("root_ready"), sem("inv_ready"), sem("normed")
        s_gp, s_gate, s_out, s_y0, s_y = sem("gate_product"), sem("gate_ready"), sem("projected"), sem("gated"), sem("y_ready")
        bank = c.bank
        block = ctx.enter_context(nc.Block())

        @block.gpsimd
        def _(pool):
            with pool.Fori(0, GROUPS) as i:
                fetch_group(c, pool, i + base, i)
                norm_pool(c, pool, i + base)

        @block.scalar
        def _(act):
            with act.Fori(0, GROUPS) as i:
                act.wait_ge(c.s_cur, i + (base + 1))
                nc.scalar.activation(o[:].rearrange("p (b t) -> p b t", b=SEQ_G), o_all[:, ds(i * SEQ_G, SEQ_G), :], ACT.Copy).then_inc(s_o, 1)
                nc.scalar.activation(pn[:], pn_all[:, ds(i * GROUP, GROUP)], ACT.Copy).then_inc(s_o, 1)
                act.wait_ge(s_o, i * 2 + 2)
                nc.scalar.activation(sq[:], o[:], ACT.Square).then_inc(s_sq, 1)
                act.wait_ge(s_sum, i + 1)
                nc.scalar.activation(root[:], bank[1], ACT.Sqrt, scale=1.0 / HD, bias=W["eps"]).then_inc(s_root, 1)
                act.wait_ge(s_gp, i + 1)
                nc.scalar.activation(gate[:].rearrange("p t d -> p (t d)"), bank[2], ACT.Sigmoid).then_inc(s_gate, 1)
                norm_scalar(c, act, i + base, ds(i * GROUP, GROUP))

        @block.tensor
        def _(pe):
            with pe.Fori(0, GROUPS) as i:
                pe.wait_ge(c.s_cur, i + (base + 1))
                for t in range(TILES):
                    sl = slice(t * P, (t + 1) * P)
                    nc.tensor.matmul(bank[2][:, sl], c.cur[:, sl], W["gate"], start=True, stop=False)
                    nc.tensor.matmul(bank[2][:, sl], c.ones[0:1, 0:P], W["bgate"][0:1], start=False, stop=True)
                    last = nc.tensor.transpose(bank[4][:, sl], c.cur[:, sl], c.ident)
                last.then_inc(s_gp, 1)
                pe.wait_ge(s_sq, i + 1)
                nc.tensor.matmul(bank[1], W["bones"], sq[:], start=True, stop=True).then_inc(s_sum, 1)
                pe.wait_ge(s_nr, i + 1)
                for t in range(TILES):
                    sl = slice(t * P, (t + 1) * P)
                    nc.tensor.matmul(bank[3][:, sl], nr[:, sl], W["out"][:, 0:P], start=True, stop=False)
                    nc.tensor.matmul(bank[3][:, sl], pn[:, sl], W["out"][:, P:2 * P], start=False, stop=False)
                    last = nc.tensor.matmul(bank[3][:, sl], c.ones[0:1, 0:P], W["bout"][0:1], start=False, stop=True)
                last.then_inc(s_out, 1)
                norm_tensor(c, pe, i + base)

        @block.vector
        def _(dve):
            rows = lambda b: bank[b].rearrange("p (t d) -> p t d", t=TILES)
            with dve.Fori(0, GROUPS) as i:
                dve.wait_ge(s_root, i + 1)
                nc.vector.reciprocal(inv[:], root[:]).then_inc(s_inv, 1)
                dve.wait_ge(s_inv, i + 1)
                nc.vector.scalar_tensor_tensor(out=nr[:], in0=o[:], scalar=W["mnorm"], in1=inv[:], op0=ALU.mult, op1=ALU.mult).then_inc(s_nr, 1)
                dve.wait_ge(s_out, i + 1)
                dve.wait_ge(s_gate, i + 1)
                nc.vector.tensor_tensor(y[:], gate[:], rows(3), ALU.mult).then_inc(s_y0, 1)
                dve.wait_ge(s_y0, i + 1)
                nc.vector.tensor_tensor(y[:], y[:], rows(4), ALU.add).then_inc(s_y, 1)
                norm_vector(c, dve, i + base, y, (s_y, i + 1))


class load_stage:
    def __init__(self, c, ctx, name):
        self.layout, width = c.layouts[name]
        self.sb = ctx.enter_context(c.nc.sbuf_tensor(f"par_{name}", [P, width], F32))
        self.sem = c.sem(f"par_{name}_loaded")
        self.src = c.params[name]

    def start(self, eng):
        eng.dma_start(self.sb[:], self.src).then_inc(self.sem, 16)

    def wait(self, eng):
        eng.wait_ge(self.sem, 16)

    def __getitem__(self, key):
        a, w = self.layout[key]
        return self.sb[:, a:a + w]


def build(nc, x_t, params, layouts, consts_layout, out):
    c = Ctx()
    c.nc, c.params, c.layouts, c.x_t, c.layer_params = nc, params, layouts, x_t, params['layers']
    with ExitStack() as ctx:
        def sb(n, shape, dt=F32): return ctx.enter_context(nc.sbuf_tensor(n, shape, dt))
        def sem(n): return ctx.enter_context(nc.semaphore(n))
        c.sem, c.attended = sem, 0
        c.attention_sems = AttentionSems(lambda n: sem("att_" + n))
        c.H = sb("H", [P, TOKENS])
        c.cur = sb("cur", [P, GROUP])
        c.stats = sb("stats", [P, TILES, 6])
        c.meanvar = sb("meanvar", [P, TILES, 2])
        c.vareps = sb("vareps", [P, TILES])
        c.rstd = sb("rstd", [P, TILES])
        c.minus_half = sb("minus_half", [P, TILES])
        c.normed = sb("normed", [P, TILES, P])
        c.ident_bf = sb("ident_bf", [P, P], BF16)
        c.scratch = sb("scratch", [P, 1])
        c.ones = sb("ones", [P, P])
        c.psum = ctx.enter_context(nc.psum_tensor("psum", [P, 8 * 512], F32))
        c.bank = [c.psum[:, b * 512:(b + 1) * 512] for b in range(8)]
        c.turned = c.bank[0]
        c.s_cur, c.s_stats, c.s_meanvar, c.s_vareps = sem("group_ready"), sem("stats_ready"), sem("meanvar_ready"), sem("vareps_ready")
        c.s_rstd, c.s_normed, c.s_turned, c.s_done = sem("rstd_ready"), sem("normed_ready"), sem("turned_ready"), sem("group_done")
        C = load_stage(c, ctx, "const")
        c.C = C
        c.ident = C["ident"]
        s_x, s_fill, s_out = sem("x_loaded"), sem("constants_filled"), sem("out_stored")
        c.s_fill = s_fill
        with nc.Block() as block:
            @block.sync
            def _(sp):
                C.start(sp)
                sp.dma_start(c.H[:], x_t).then_inc(s_x, 16)
                sp.wait_ge(s_x, 16)
                C.wait(sp)

            @block.vector
            def _(dve):
                C.wait(dve)
                nc.vector.tensor_copy(c.ident_bf[:], c.ident)
                dve.wait_ge(s_x, 16)
                nc.vector.memset(c.minus_half[:], -0.5).then_inc(c.s_done, 1)
                nc.vector.memset(c.ones[:], 1.0).then_inc(s_fill, 1)
                dve.wait_ge(s_fill, 1)
        base = 0
        for stage in (encoder, experts, delta_rule, fp4_network, linear_attention, ternary_network, rope_attention, fft_mix):
            base = stage(c, base)
        with nc.Block() as block:
            @block.sync
            def _(sp):
                sp.wait_ge(c.s_done, base + 1)
                sp.dma_start(out, c.H[:]).then_inc(s_out, 16)
                sp.wait_ge(s_out, 16)



def _pack(parts):
    layout, at = {}, 0
    for name, a in parts.items():
        layout[name] = (at, a.shape[1])
        at += a.shape[1]
    packed = np.zeros((P, at), np.float32)
    for name, a in parts.items():
        packed[:a.shape[0], layout[name][0]:layout[name][0] + a.shape[1]] = a
    return packed, layout, at


def _host(inp):
    out = {}
    j = np.arange(D)
    ang = 2 * np.pi * ((j[:, None] * j[None, :]) % D) / D
    fr, fi = np.cos(ang), -np.sin(ang)
    out["const"] = {"ident": np.eye(P)}
    out["s8"] = {"wr": inp["L3_ffn_w_freq_real"], "wi": inp["L3_ffn_w_freq_imag"], "fr": fr, "fi": fi, "nfi": -fi,
                 "gr": fr / D, "ngi": fi / D, "bias": inp["L3_ffn_bias"][None, :]}

    def pad_cols(w):
        a = np.zeros(w.shape[:-1] + (HT, 4, 32), w.dtype)
        a[..., 1:VW] = w.reshape(w.shape[:-1] + (HT, 4, HD))
        return a.reshape(w.shape[:-1] + (HT * P,))

    def swap(w):
        return w.reshape(w.shape[:-1] + (D // 2, 2))[..., ::-1].reshape(w.shape)

    idx = np.arange(S)
    neg = -1e30

    def mask_tables(seen):
        add = np.where(seen, 0.0, neg)
        q = np.broadcast_to(add.reshape(JT, P, S).transpose(1, 0, 2)[:, :, None, :], (P, JT, 2, S))
        k = np.broadcast_to(add.T.reshape(JT, P, S).transpose(1, 0, 2)[:, :, None, :], (P, JT, 2, S))
        return np.stack([q, k], 1).reshape(P, -1)

    causal = idx[None, :] <= idx[:, None]
    half = HD // 2
    inv = (10000.0 ** (-np.arange(half, dtype=np.float32) * 2.0 / HD)).astype(np.float32)
    rang = (idx.astype(np.float32)[:, None] * inv[None, :]).astype(np.float32)
    rot = np.zeros((2, 2, 32, S))
    for d in range(HD):
        rot[:, 0, 1 + d] = np.cos(rang[:, d // 2])
        rot[:, 1, 1 + d] = np.sin(rang[:, d // 2]) * (-1 if d % 2 == 0 else 1)
    rot[0] *= HD ** -0.5
    rot = np.tile(rot, (1, 1, 4, SEQ_G)).transpose(2, 0, 1, 3)
    row0 = np.zeros((P, 2)); row0[::32, 1] = 1.0
    wq, wk, wv, wo = (inp["L3_attn_" + n].T for n in ("Wq", "Wk", "Wv", "Wo"))
    wqk = np.concatenate([pad_cols(wq), pad_cols(swap(wq)), pad_cols(wk), pad_cols(swap(wk))], 1)
    heads4 = (np.arange(P)[:, None] // 32 == np.arange(4)[None, :]).astype(np.float32)
    i32 = (idx[:, None] & idx[None, :]) == 0
    zero = (~i32).astype(np.float32).T.reshape(JT, P, S).transpose(1, 0, 2).reshape(P, -1)
    floor = np.zeros((P, JT))
    floor[0, 0] = 2 * neg
    level = np.frexp((idx + 1).astype(np.float64))[1] - 1
    coord = (idx >> level) / 2.0 ** level
    div = np.exp(np.arange(0, D, 2, dtype=np.float64) * -(np.log(10000.0) / D))
    pang = idx[:, None].astype(np.float64) * div[None, :]
    pos = np.zeros((S, D), np.float32)
    pos[:, 0::2] = np.sin(pang) * coord[:, None]
    pos[:, 1::2] = np.cos(pang) * coord[:, None]
    col = lambda a: a.reshape(-1, P).T
    g = lambda n: inp["L0_attn_" + n]
    out["s1"] = {"neg": mask_tables(i32), "zero": zero, "floor": floor, "pos": pos.T,
                 "heads": heads4, "gf": col(g("lnf_g")), "bf": col(g("lnf_b"))}
    for l in range(LAYERS):
        bk = pad_cols(g("bk")[l])
        bk[::32] = 1.0
        bk4 = np.zeros((HT, 4, 4, 32), bk.dtype)
        for copy in range(4):
            bk4[:, copy, copy] = bk.reshape(HT, 4, 32)[:, copy]
        out[f"layer{l}"] = {"wq": pad_cols(g("Wq")[l]), "wk": pad_cols(g("Wk")[l]), "wv": g("Wv")[l], "wo": g("Wo")[l],
                            "w1": g("W1")[l], "w2": g("W2")[l].reshape(4, P, D).transpose(1, 0, 2).reshape(P, -1),
                            "bq": col(pad_cols(g("bq")[l])), "bk": bk4.reshape(HT * 4, P).T, "bv": g("bv")[l][None], "bo": g("bo")[l][None],
                            "b1": col(g("b1")[l]), "b2": g("b2")[l][None], "g1": col(g("ln1_g")[l]), "be1": col(g("ln1_b")[l]),
                            "g2": col(g("ln2_g")[l]), "be2": col(g("ln2_b")[l])}
    m = lambda n: inp["L0_ffn_" + n]
    w1 = np.concatenate([m("shared_w1")[None], m("experts_w1")])
    w2 = np.concatenate([m("shared_w2")[None], m("experts_w2")])
    e8 = np.arange(EXPERTS)
    out["s2"] = {"w1": w1.transpose(2, 0, 1).reshape(P, -1),
                 "w2": w2.transpose(2, 0, 1).reshape(FC, P, EXPERTS + 1, D).transpose(1, 2, 0, 3).reshape(P, -1),
                 "gate": m("gate_w").T,
                 "before": np.broadcast_to((e8[None, :] < e8[:, None]).reshape(1, -1), (P, EXPERTS * EXPERTS))}
    d1 = lambda n: inp["L1_attn_" + n]
    ctrl, cb = d1("ctrl_W"), d1("ctrl_b")
    rep = lambda a: np.repeat(a, HD, axis=-1)
    h_of, r_of = np.arange(P) // HD, np.arange(P) % HD
    bones = (h_of[:, None] == h_of[None, :]).astype(np.float32)
    spread = np.stack([bones * (r_of[:, None] == v) for v in range(HD)], 1)
    gather = np.stack([bones * (r_of[None, :] == v) for v in range(HD)], 1)
    partner = np.zeros((P, P))
    for a in range(0, P, 2):
        partner[a + 1, a] = 1.0
        partner[a, a + 1] = -1.0
    out["s3"] = {"theta": col(np.repeat(d1("p20_theta"), 2)), "decay": col(np.repeat(d1("p20_decay_log"), 2)),
                 "partner": partner, "ctrl": ctrl[:, 0:3 * D], "dec": rep(ctrl[:, 3 * D:3 * D + HEADS]),
                 "beta": rep(ctrl[:, 3 * D + HEADS:3 * D + 2 * HEADS]), "gate": ctrl[:, 3 * D + 2 * HEADS:],
                 "bctrl": np.stack([cb[0:D], cb[D:2 * D], cb[2 * D:3 * D], rep(cb[3 * D:3 * D + HEADS]),
                                    rep(cb[3 * D + HEADS:3 * D + 2 * HEADS])], 1),
                 "bgate": cb[3 * D + 2 * HEADS:][None], "p20c": d1("p20c_W"),
                 "conv": np.concatenate([d1("qconv_w"), d1("kconv_w"), d1("vconv_w")], 1),
                 "vnorm": col(d1("vnorm_scale")), "mnorm": col(np.tile(d1("mnorm_scale"), HEADS)), "ramp": col(d1("ramp_logit")),
                 "out": np.concatenate([d1("out_W")[0:D], d1("out_W")[D:]], 1), "bout": d1("out_b")[None],
                 "eps": np.full((P, 1), 1e-6), "time": np.broadcast_to(idx[None, :], (P, S)), "bones": bones, "minus_bones": -bones,
                 "spread": spread.reshape(P, -1), "gather": gather.reshape(P, -1)}
    f4 = lambda n: inp["L1_ffn_" + n]
    rows4 = lambda w: np.concatenate([w, np.zeros((FF4P - FF4, D), w.dtype)]).reshape(3, P, D).transpose(1, 0, 2).reshape(P, -1)
    out["s4"] = {"w": np.concatenate([rows4(f4("w_gate")), rows4(f4("w_up")), f4("w_down"), np.zeros((D, FF4P - FF4), np.float32)], 1)}
    l2 = lambda n: inp["L2_attn_" + n]
    wepad = np.zeros((LAT, HT, 4, 32), np.float32)
    wepad[..., 1:VW] = l2("We").reshape(LAT, HT, 1, HD)
    off = np.zeros((P, 1)); off.reshape(4, 32)[:, 0] = -1e4; off.reshape(4, 32)[:, VW:] = -1e4
    out["s5"] = {"wq": pad_cols(l2("Wq")), "bq": col(pad_cols(l2("bq"))), "wkv": np.concatenate([l2("Wk"), l2("Wv")], 1),
                 "bkv": np.stack([l2("bk"), l2("bv")], 1), "wc": l2("Wc"), "we": l2("We"), "wepad": wepad.reshape(LAT, -1),
                 "wo": l2("Wo"), "bo": l2("bo")[None], "heads": heads4, "gamma": col(l2("gamma")), "beta": col(l2("beta")), "off": off,
                 "tri": causal.T.reshape(JT, P, S).transpose(1, 0, 2).reshape(P, -1)}
    t = lambda n: inp["L2_ffn_" + n]
    chunked = lambda w: w.T.reshape(FC, P, -1).transpose(1, 0, 2).reshape(P, -1)
    out["s6"] = {"w1": t("w1_w").T, "w2": t("w2_w").T, "h1": chunked(t("h1_w")), "h2": chunked(t("h2_w")), "w3": chunked(t("w3_w")),
                 "s1": col(t("w1_s")), "s2": col(t("w2_s")), "hs": np.concatenate([col(t("h1_s")), col(t("h2_s"))], 1), "s3": col(t("w3_s"))}
    out["s7"] = {"wqk": wqk, "wv": wv, "wo": wo, "rot": rot.reshape(P, -1), "heads": heads4, "row": row0[:, 1:2], "neg": mask_tables(causal),
                 "floor": np.full((P, JT), 2 * neg)}
    return out


def kernel(**inputs):
    import concourse.bacc as _bacc
    from concourse import mybir as _mybir
    from concourse.bass_utils import run_bass_kernel_spmd as _run

    inp = {k: np.asarray(v) for k, v in inputs.items()}
    nc = _bacc.Bacc("TRN2", target_bir_lowering=False, num_devices=1)
    arrays, params, layouts = {}, {}, {}

    def dram(name, a):
        a = np.ascontiguousarray(a)
        arrays[name] = a
        return nc.dram_tensor(name, a.shape, _mybir.dt.from_np(a.dtype), kind="ExternalInput").ap()

    x_t = dram("x_t", inp["L0_attn_x"].reshape(TOKENS, D).T)
    layers = []
    for name, parts in _host(inp).items():
        packed, layout, width = _pack(parts)
        layouts[name] = (layout, width)
        if name.startswith("layer"):
            layers.append(packed)
            params[name] = None
        else:
            params[name] = dram("par_in_" + name, packed)
    params["layers"] = dram("par_in_layers", np.stack(layers))
    out = nc.dram_tensor("out_t", (D, TOKENS), _mybir.dt.float32, kind="ExternalOutput").ap()
    build(nc, x_t, params, layouts, None, out)
    r = _run(nc, [arrays], core_ids=[0])
    return np.ascontiguousarray(r.results[0]["out_t"].T).reshape(SEQS, S, D)
```
